# Optimizing a Trainium2 kernel written in Bass

```python
import numpy as np
import jax
import jax.numpy as jnp

def _softmax(x, axis=-1):
    return jax.nn.softmax(x, axis=axis)

def _gelu(x):
    return jax.nn.gelu(x, approximate=True)

def _silu(x):
    return jax.nn.silu(x)

def _sigmoid(x):
    return jax.nn.sigmoid(x)

def _layernorm(x, axis=-1, eps=1e-05):
    m = jnp.mean(x, axis=axis, keepdims=True)
    v = jnp.var(x, axis=axis, keepdims=True)
    return (x - m) / jnp.sqrt(v + eps)

def _scatter_add(tgt, idx, src, axis=0):
    return tgt.at[idx].add(src)

def _segment_sum(src, seg, n):
    return jax.ops.segment_sum(src, seg, n)
kernel_name = 'mk_adj_ffn_d1_adj_r2_e5c3f9'

def setup_inputs(seed: int=0):
    np.random.seed(seed)
    _w = jnp.asarray

    def _rec_inputs():
        import jax
        import jax.numpy as jnp
        _gk = jax.random.key(seed)
        x = -0.0002928 + 1 * jax.random.normal(jax.random.fold_in(_gk, 1), (2048, 512), jnp.float32)
        _w = (1.0 + jnp.arange(2048, dtype=jnp.float32)) ** (-0.5)
        _w = _w / _w.mean()
        _pij = jnp.clip(0.0078125 * _w[:, None] * _w[None, :], 0.0, 1.0)
        _a = jax.random.uniform(jax.random.fold_in(_gk, 2), (2048, 2048)) < _pij
        _af = _a.astype(jnp.float32)
        adj = _af
        return (x, adj)
    x, adj = _rec_inputs()

    def _L0_gnn_setup():
        import jax, jax.numpy as jnp
        import numpy as np
        N = 2048
        D_IN = 512
        H = 16
        DH = D_IN // H
        ALPHA = 0.2
        MASK_VAL = -65500.0
        key = jax.random.key(seed)
        ks = jax.random.split(key, 7)
        x = jax.random.normal(ks[0], (N, D_IN), dtype=jnp.float32)
        adj = jax.random.randint(ks[1], (N, N), 0, 2).astype(jnp.float32)
        s = 1.0 / np.sqrt(D_IN)
        W_seq = jax.random.normal(ks[2], (D_IN, D_IN), dtype=jnp.float32) * s
        a1 = jax.random.normal(ks[3], (DH,), dtype=jnp.float32) / np.sqrt(DH)
        a2 = jax.random.normal(ks[4], (DH,), dtype=jnp.float32) / np.sqrt(DH)
        W_out = jax.random.normal(ks[5], (D_IN, D_IN), dtype=jnp.float32) * s
        b_out = jax.random.normal(ks[6], (D_IN,), dtype=jnp.float32) * 0.01
        return {'x': x, 'adj': adj, 'W_seq': W_seq, 'a1': a1, 'a2': a2, 'W_out': W_out, 'b_out': b_out}
    _L0_gnn_all = _L0_gnn_setup()
    _L0_gnn_in = {k: v for k, v in _L0_gnn_all.items() if k in ('W_seq', 'a1', 'a2', 'W_out', 'b_out')}
    del _L0_gnn_all

    def _L0_ffn_setup():
        import jax, jax.numpy as jnp
        import numpy as np
        NUM_EXPERTS = 8
        CAPACITY_FACTOR = 1.0
        key = jax.random.key(seed)
        k1, k2, k3, k4 = jax.random.split(key, 4)
        B, S, D, E, F = (8, 1024, 512, NUM_EXPERTS, 2048)
        x = jax.random.normal(k1, (B, S, D), dtype=jnp.float32)
        router_w = jax.random.normal(k2, (D, E), dtype=jnp.float32) * D ** (-0.5)
        w1 = jax.random.normal(k3, (E, D, F), dtype=jnp.float32) * D ** (-0.5)
        w2 = jax.random.normal(k4, (E, F, D), dtype=jnp.float32) * F ** (-0.5)
        return {'x': x, 'router_w': router_w, 'w1': w1, 'w2': w2}
    _L0_ffn_all = _L0_ffn_setup()
    _L0_ffn_in = {k: v for k, v in _L0_ffn_all.items() if k in ('router_w', 'w1', 'w2')}
    del _L0_ffn_all
    return {'x': x, 'adj': adj, 'L0_gnn_W_seq': _L0_gnn_in['W_seq'], 'L0_gnn_a1': _L0_gnn_in['a1'], 'L0_gnn_a2': _L0_gnn_in['a2'], 'L0_gnn_W_out': _L0_gnn_in['W_out'], 'L0_gnn_b_out': _L0_gnn_in['b_out'], 'L0_ffn_router_w': _L0_ffn_in['router_w'], 'L0_ffn_w1': _L0_ffn_in['w1'], 'L0_ffn_w2': _L0_ffn_in['w2']}

def reference(x, adj, L0_gnn_W_seq, L0_gnn_a1, L0_gnn_a2, L0_gnn_W_out, L0_gnn_b_out, L0_ffn_router_w, L0_ffn_w1, L0_ffn_w2):
    import jax
    import jax.numpy as jnp

    def _L0_gnn_ref(x, adj, W_seq, a1, a2, W_out, b_out):
        import jax, jax.numpy as jnp
        import numpy as np
        N = 2048
        D_IN = 512
        H = 16
        DH = D_IN // H
        ALPHA = 0.2
        MASK_VAL = -65500.0
        seq = (x @ W_seq).reshape(N, H, DH)
        score1 = jnp.einsum('nhd,d->hn', seq, a1)
        score2 = jnp.einsum('nhd,d->hn', seq, a2)
        scores = score1[:, :, None] + score2[:, None, :]
        scores = jax.nn.leaky_relu(scores, negative_slope=ALPHA)
        scores = scores + (1.0 - adj)[None, :, :] * MASK_VAL
        attn = jax.nn.softmax(scores, axis=-1)
        hidden = jnp.einsum('hij,jhd->ihd', attn, seq).reshape(N, D_IN)
        hidden = hidden @ W_out + b_out
        return jax.nn.elu(hidden)

    def _L0_ffn_ref(x, router_w, w1, w2):
        import jax, jax.numpy as jnp
        import numpy as np
        NUM_EXPERTS = 8
        CAPACITY_FACTOR = 1.0
        B, S, D = x.shape
        E = router_w.shape[1]
        T = B * S
        C = int(CAPACITY_FACTOR * T / E)
        x_flat = x.reshape(T, D)
        logits = x_flat @ router_w
        probs = jax.nn.softmax(logits, axis=-1)
        expert_idx = jnp.argmax(probs, axis=-1)
        gate = jnp.take_along_axis(probs, expert_idx[:, None], axis=1)[:, 0]
        onehot = jax.nn.one_hot(expert_idx, E, dtype=jnp.float32)
        pos_all = jnp.cumsum(onehot, axis=0) - 1.0
        pos = jnp.take_along_axis(pos_all, expert_idx[:, None], axis=1)[:, 0]
        pos = pos.astype(jnp.int32)
        keep = (pos < C).astype(x_flat.dtype)
        pos_c = jnp.clip(pos, 0, C - 1)
        expert_in = jnp.zeros((E, C, D), dtype=x_flat.dtype)
        expert_in = expert_in.at[expert_idx, pos_c].add(x_flat * keep[:, None])
        hidden = jax.nn.gelu(jnp.einsum('ecd,edf->ecf', expert_in, w1))
        expert_out = jnp.einsum('ecf,efd->ecd', hidden, w2)
        y = expert_out[expert_idx, pos_c] * (gate * keep)[:, None]
        return y.reshape(B, S, D)
    x = x + _L0_gnn_ref(_layernorm(x, axis=-1), adj, L0_gnn_W_seq, L0_gnn_a1, L0_gnn_a2, L0_gnn_W_out, L0_gnn_b_out)
    x = x + _L0_ffn_ref(_layernorm(x, axis=-1)[None], L0_ffn_router_w, L0_ffn_w1, L0_ffn_w2)[0]
    return x

_drawn_inputs = setup_inputs


def setup_inputs(seed=0):
    import zlib

    import numpy as np

    out = dict(_drawn_inputs(seed))
    spreads = {}
    factors = {'L0_gnn_b_out': 4.136}
    for name, (base, spread) in spreads.items():
        noise = np.random.default_rng([zlib.crc32(name.encode()), seed]).standard_normal(out[name].shape)
        drawn = base * np.exp(spread * noise) if base else spread * noise
        out[name] = jnp.asarray(drawn.astype(out[name].dtype))
    for name, factor in factors.items():
        out[name] = (out[name] * factor).astype(out[name].dtype)
    return out
```

```python
from contextlib import ExitStack

import concourse.bass as bass
from concourse import mybir

ALU = mybir.AluOpType
ACT = mybir.ActivationFunctionType
AX = mybir.AxisListType
F32 = mybir.dt.float32
BF16 = mybir.dt.bfloat16
F16 = mybir.dt.float16
I32 = mybir.dt.int32
U8 = mybir.dt.uint8
F8 = mybir.dt.float8e4
U32 = mybir.dt.uint32

P = 128
EPS = 1e-5
ALPHA = 0.2
LO = 2048.0
SHIFT = 256.0
STEEP = 2.0 ** 100
EDGE = 112.0
OFF = 4096
DVE_TILES = (2, 5, 7, 10, 12, 15)


def live(t, back, tiles):
    return not isinstance(t, int) or 0 <= t - back < tiles


def wait(eng, sem, count):
    if not isinstance(count, int) or count > 0:
        eng.wait_ge(sem, count)


class Steps:

    def __init__(self, eng, sem):
        self.eng, self.sem, self.base, self.n = eng, sem, 0, 0

    def done(self, ins):
        ins.then_inc(self.sem, 1)
        self.n += 1
        self.eng.wait_ge(self.sem, self.base + self.n)


def in_pairs(eng, tiles, first, last, body, steps=None, per=0):
    for t in range(first):
        body(t, t % 2)
    loops = (tiles - first) // 2
    if steps:
        start, steps.n, before = steps.base, 0, steps.n
        start = start + before
    with eng.Fori(0, loops) as i:
        for k in range(2):
            if steps:
                steps.base, steps.n = start + i * (2 * per) + k * per, 0
            body(i * 2 + (first + k), k)
            assert not steps or steps.n == per, (steps.n, per)
    if steps:
        steps.base, steps.n = start + loops * 2 * per, 0
    for t in range(tiles, last):
        body(t, t % 2)


def gnn_moe(nc, x, adj, W_seq, a1, a2, W_out, b_out, router_w, w1, w2, out):
    N, D = x.shape
    DH = a1.shape[0]
    H = D // DH
    E, _, F = w1.shape
    C = N // E
    T = N // P
    DK = D // P
    FT = F // P
    CT = C // P
    DC = DH + 1
    VC = 2 * DC
    ROW = D + 4
    ACT_TILES = [j for j in range(T) if j not in DVE_TILES]
    NT, NM = 5, 8
    assert len(ACT_TILES) % NT == 0 and T % NM == 0

    s1T_dram = nc.dram_tensor("s1T_dram", (H, N), F32, kind="Internal").ap()
    slots_dram = nc.dram_tensor("slots_dram", (E * C, ROW), F32, kind="Internal").ap()

    with ExitStack() as ctx:
        def sem(name):
            return ctx.enter_context(nc.semaphore(name))

        CONST = 14336
        SIZE = 212608
        arena = ctx.enter_context(nc.sbuf_tensor("arena", [P, SIZE // 4], F32))
        cursor = [0]
        start_of = {}

        def at(offset, name, shape, dt):
            size = {F32: 4, I32: 4, U32: 4, BF16: 2, F16: 2, U8: 1, F8: 1}[dt]
            n = size
            for s in shape[1:]:
                n *= s
            start_of[name] = offset
            cursor[0] = offset + (n + 31) // 32 * 32
            assert cursor[0] <= SIZE, (name, cursor[0])
            return nc.alloc_sbuf_tensor_at(name, shape, dt, offset=ARENA + offset)

        def after(name, shape, dt):
            return at(cursor[0], name, shape, dt)

        ARENA = 16512

        ident = at(0, "ident", [P, P], F32)
        ident_b = after("ident_b", [P, P], BF16)
        ones = after("ones", [H, P], F32)
        ones_b = after("ones_b", [P, P], BF16)
        earlier_b = after("earlier_b", [P, P], BF16)
        a_bc = after("a_bc", [P, 2, DH], F32)
        scores = after("scores", [P, T, 2 * H], F32)
        uu = after("uu", [P, H, T, 2], F32)
        uuV = after("uuV", [P, H, T, 2], F32)
        AA = after("AA", [P, H, T, 2], F32)
        neg_b = after("neg_b", [P, H, T], F32)
        steep_b = after("steep_b", [P, H, T], F32)
        steep_now = after("steep_now", [P, 2, T], F32)
        bmax = after("bmax", [P, H], F32)
        bmaxT = after("bmaxT", [H, 1], F32)
        bdiag = after("bdiag", [H, H], F32)
        B_bc = after("B_bc", [P, H], F32)
        stats = after("stats", [P, 2, 6], F32)
        mean = after("mean", [P, 2], F32)
        tile_stats = after("tile_stats", [P, T, 6], F32)
        rstd = after("rstd", [P, T], F32)
        newton = [after(f"newton{k}", [P, T], F32) for k in range(2)]
        deg = after("deg", [P, 2], F32)
        lonely = after("lonely", [P, 2], F32)
        router_sb = after("router_sb", [P, DK, E], F32)
        rden = after("rden", [P, 2, H], F32)
        logits = after("logits", [P, T, E], F32)
        rank8 = after("rank8", [P, E], F32)
        first8 = after("first8", [P, E], F32)
        rank8_i = after("rank8_i", [P, E], I32)
        first8_i = after("first8_i", [P, E], I32)
        slot_i = after("slot_i", [P, T], U32)
        assert cursor[0] <= CONST, cursor[0]

        adjT = at(CONST, "adjT", [P, T, N], U8)
        above = [after(f"above{k}", [P, N], U8) for k in range(2)]
        hid = at(CONST + T * N * 2, "hid", [P, T, H, DC], F32)
        tables = [after(f"tables{k}", [P, T, 3 * VC], F16) for k in range(2)]
        value = after("value", [P, T, VC], F32)
        both = after("both", [P, T, VC], F32)
        seq = after("seq", [P, T, D], F32)
        a_row = [after(f"a_row{k}", [P, N], F32) for k in range(2)]
        relus = [after(f"relu{k}", [P, N], F8) for k in range(NT)]
        masks = [after(f"mask{k}", [P, N], U8) for k in range(NM)]

        adj_in = [at(start_of["hid"], "adj_in0", [P, N], F32), after("adj_in1", [P, N], F32)]
        adj_b = [after(f"adj_b{k}", [P, N], BF16) for k in range(2)]
        x_in = [after(f"x_in{k}", [P, D], F32) for k in range(2)]
        xn = [after(f"xn{k}", [P, D], F32) for k in range(2)]
        assert cursor[0] <= start_of["tables0"] 
        slot_init = at(start_of["tables0"], "slot_init", [P, ROW], F32)
        wseq_sb = at(start_of["a_row0"], "wseq_sb", [P, DK, D], F32)
        w_times_a = after("w_times_a", [P, 2, DK, D // 2], F32)
        xnT = [after(f"xnT{k}", [P, DK, P], F32) for k in range(2)]
        w_score = after("w_score", [P, DK, 2 * H], F32)
        assert cursor[0] <= start_of["mask0"]
        s1T = at(start_of["mask0"], "s1T", [H, N], F32)
        sumB = [after(f"sumB{k}", [P, H, T], F32) for k in range(6)]

        rows = at(CONST, "rows", [P, T, ROW], F32)
        wout_sb = after("wout_sb", [P, DK, D], F32)
        bout_bc = after("bout_bc", [P, D], F32)
        heads = [after(f"heads{k}", [P, D], F32) for k in range(2)]
        headsT = [after(f"headsT{k}", [P, DK, P], F32) for k in range(2)]
        z = [after(f"z{k}", [P, D], F32) for k in range(2)]
        xn2 = [after(f"xn2_{k}", [P, D], F32) for k in range(2)]
        xn2T = [after(f"xn2T{k}", [P, DK, P], F32) for k in range(2)]
        assert cursor[0] <= start_of["hid"], (cursor[0], start_of["hid"])

        w1_sb = [at(start_of["seq"], "w1_sb0", [P, DK, F], F32)]
        w2_sb = [after("w2_sb0", [P, FT, D], F32)]
        w1_sb.append(at(start_of["wout_sb"], "w1_sb1", [P, DK, F], F32))
        w2_sb.append(after("w2_sb1", [P, FT, D], F32))
        assert cursor[0] <= start_of["tables0"], (cursor[0], start_of["tables0"])
        slot_rows = [at(start_of["tables0"], "slot_rows0", [P, ROW], F32)]
        slot_rows += [after(f"slot_rows{k}", [P, ROW], F32) for k in range(1, 2 * CT)]
        slot_xn = [after(f"slot_xn{k}", [P, D], F32) for k in range(CT)]
        y = [after(f"y{k}", [P, D], F32) for k in range(CT)]
        ez = [after(f"ez{k}", [P, D], F32) for k in range(2)]
        assert cursor[0] <= start_of["seq"], (cursor[0], start_of["seq"])
        xT = [at(CONST, "xT0", [P, DK, C], F32), after("xT1", [P, DK, C], F32)]
        hT = after("hT", [P, FT, C], F32)
        assert cursor[0] <= start_of["wout_sb"]
        rt = [at(start_of["heads0"] + 512 * k, f"rt{k}", [P, T, E], F32) for k in range(8)]
        rt1 = [at(start_of["heads0"] + 4096 + 64 * k, f"rt1_{k}", [P, T], F32) for k in range(6)]
        cum_b = at(start_of["heads0"] + 4608, "cum_b", [P, T, E], BF16)
        oh_b = at(start_of["heads0"] + 4864, "oh_b", [P, T, E], BF16)

        ps = ctx.enter_context(nc.psum_tensor("ps", [P, 8, 512], F32))
        node_ps = ps[:, :, :].rearrange("p b (i c) -> p (b i) c", i=2)

        pool_step, dve_step = sem("pool_step"), sem("dve_step")
        consts = sem("consts")
        wseq_in, a_in, slot_init_out = sem("wseq_in"), sem("a_in"), sem("slot_init_out")
        x_loaded = [sem(f"x_loaded{k}") for k in range(2)]
        adj_loaded = [sem(f"adj_loaded{k}") for k in range(2)]
        wa_products, wa_ready = sem("wa_products"), sem("wa_ready")
        xn_ready, deg_ready, adjb_ready = sem("xn_ready"), sem("deg_ready"), sem("adjb_ready")
        xn_turned, adj_turned0, adj_turned1 = sem("xn_turned"), sem("adj_turned0"), sem("adj_turned1")
        xnT_ready, adjT_half0, adjT_half1 = sem("xnT_ready"), sem("adjT_half0"), sem("adjT_half1")
        seq_product, seq_ready = sem("seq_product"), sem("seq_ready")
        s1_turned, s1T_ready, s1T_out = sem("s1_turned"), sem("s1T_ready"), sem("s1T_out")
        bmax_ready, bmax_turned = sem("bmax_ready"), sem("bmax_turned")
        bdiag_ready, bmax_spread = sem("bdiag_ready"), sem("bmax_spread")
        var_ready, dev_ready = sem("var_ready"), sem("dev_ready")
        args_ready, exps_ready, factors_ready = sem("args_ready"), sem("exps_ready"), sem("factors_ready")
        a_row_in = [sem(f"a_row_in{k}") for k in range(2)]
        relu_ready, above_ready = sem("relu_ready"), sem("above_ready")
        mask_ready, mask_used = sem("mask_ready"), sem("mask_used")
        value_ready, table_ready = sem("value_ready"), sem("table_ready")
        head_summed, lo_ready, sums_free = sem("head_summed"), sem("lo_ready"), sem("sums_free")
        head_done = sem("head_done")
        post_in, rows_in = sem("post_in"), sem("rows_in")
        heads_ready, heads_turned, headsT_ready = sem("heads_ready"), sem("heads_turned"), sem("headsT_ready")
        proj_product, z_ready, ez_ready = sem("proj_product"), sem("z_ready"), sem("ez_ready")
        xn2_ready, xn2_turned, xn2T_ready = sem("xn2_ready"), sem("xn2_turned"), sem("xn2T_ready")
        logit_product, logits_ready, x1_out = sem("logit_product"), sem("logits_ready"), sem("x1_out")
        top_gap, top_exp, onehot_ready = sem("top_gap"), sem("top_exp"), sem("onehot_ready")
        counts_ready, slots_ready, scattered = sem("counts_ready"), sem("slots_ready"), sem("scattered")
        token_number = sem("token_number")
        waited = sem("waited")
        w_in = [[sem(f"w{m}_in{k}") for k in range(2)] for m in (1, 2)]
        slot_in = [sem(f"slot_in{k}") for k in range(2)]
        sx_ready, sx_turned, xT_ready = sem("sx_ready"), sem("sx_turned"), sem("xT_ready")
        h_product, h_ready, y_product, y_ready = sem("h_product"), sem("h_ready"), sem("y_product"), sem("y_ready")
        y_out = [sem(f"y_out{c}") for c in range(CT)]

        def wait_apart(eng, sem, count):
            wait(eng, sem, count)
            if not isinstance(count, int):
                eng.sem_inc(waited, 1)

        block = ctx.enter_context(nc.Block())

        @block.sync
        def _(sp):
            sp.dma_start(wseq_sb[:], W_seq.rearrange("(k p) n -> p k n", p=P)).then_inc(wseq_in, 16)
            for i, a in enumerate((a1, a2)):
                sp.dma_start(a_bc[:, i, :], a.rearrange("(o d) -> o d", o=1).broadcast_to([P, DH])).then_inc(a_in, 16)
            sp.dma_start(router_sb[:], router_w.rearrange("(k p) e -> p k e", p=P)).then_inc(a_in, 16)

            def load(t, k):
                wait(sp, xn_ready, t - 1)
                sp.dma_start(x_in[k][:], x[bass.ds(t * P, P), :]).then_inc(x_loaded[k], 16)
                wait(sp, deg_ready, t - 1)
                sp.dma_start(adj_in[k][:], adj[bass.ds(t * P, P), :]).then_inc(adj_loaded[k], 16)
            in_pairs(sp, T, 2, T, load)

            sp.wait_ge(consts, 8)
            sp.dma_start(slots_dram.rearrange("(n p) r -> p n r", p=P),
                         slot_init[:].unsqueeze(1).broadcast_to([P, T, ROW])).then_inc(slot_init_out, 16)
            sp.wait_ge(s1T_ready, 4)
            sp.dma_start(s1T_dram, s1T[:]).then_inc(s1T_out, 16)
            sp.wait_ge(s1T_out, 16)
            sp.wait_ge(slot_init_out, 16)
            sp.wait_ge(seq_ready, T)

            def load_a(h, k):
                wait(sp, mask_ready, (h - 1) * T)
                sp.dma_start(a_row[k][:], s1T_dram[bass.ds(h, 1), :].broadcast_to([P, N])).then_inc(a_row_in[k], 16)
            in_pairs(sp, H, 2, H, load_a)

            sp.wait_ge(head_summed, 2 * H)
            for t in range(T):
                sp.dma_start(rows[:, t, 0:D], x[t * P:(t + 1) * P, :]).then_inc(rows_in, 16)
                if t == 0:
                    sp.dma_start(wout_sb[:], W_out.rearrange("(k p) n -> p k n", p=P)).then_inc(post_in, 16)
                    sp.dma_start(bout_bc[:], b_out.rearrange("(o d) -> o d", o=1).broadcast_to([P, D])).then_inc(post_in, 16)

            def load_w(e, k):
                sp.dma_start(w1_sb[k][:], w1[bass.ds(e, 1), :, :].rearrange("o (k p) f -> p (o k) f", p=P)).then_inc(w_in[0][k], 16)
                sp.dma_start(w2_sb[k][:], w2[bass.ds(e, 1), :, :].rearrange("o (k p) d -> p (o k) d", p=P)).then_inc(w_in[1][k], 16)
            load_w(0, 0)

            def store(t, k):
                sp.wait_ge(xn2_ready, t + 1)
                sp.dma_start(out[bass.ds(t * P, P), :], rows[:, bass.ds(t, 1), 0:D].rearrange("p o d -> p (o d)")).then_inc(x1_out, 16)
            in_pairs(sp, T, 2, T, store)
            sp.wait_ge(scattered, 16 * T)
            sp.wait_ge(logits_ready, T)
            load_w(1, 1)

            def load_slots(e, k):
                for c in range(CT):
                    wait(sp, y_out[c], 16 * (e - 1))
                for c in range(CT):
                    sp.dma_start(slot_rows[CT * k + c][:], slots_dram[bass.ds(e * C + c * P, P), :]).then_inc(slot_in[k], 16)
            load_slots(0, 0)
            load_slots(1, 1)

            def refill(e, k):
                load_slots(e, k)
                sp.wait_ge(y_product, CT * (e - 1))
                load_w(e, k)
            in_pairs(sp, E, 2, E, lambda e, k: refill(e, k) if not isinstance(e, int) else None)
            sp.wait_ge(x1_out, 16 * T)

        @block.gpsimd
        def _(pool):
            pool.memset(ident[:], 0.0).then_inc(pool_step, 1)
            pool.memset(ones_b[:], 1.0).then_inc(consts, 1)
            pool.memset(ones[:], 1.0).then_inc(consts, 1)
            pool.memset(slot_init[:], 0.0).then_inc(pool_step, 1)
            pool.wait_ge(pool_step, 2)
            pool.affine_select(out=ident[:], in_=ident[:], compare_op=ALU.not_equal, fill=1.0, base=0,
                               pattern=[[-1, P]], channel_multiplier=1).then_inc(consts, 1)
            pool.memset(slot_init[:].bitcast(I32)[:, D + 1:D + 2], OFF).then_inc(consts, 1)
            pool.wait_ge(consts, 3)
            pool.tensor_copy(ident_b[:], ident[:]).then_inc(consts, 1)
            pool.affine_select(out=earlier_b[:], in_=ones_b[:], compare_op=ALU.is_gt, fill=0.0, base=0,
                               pattern=[[1, P]], channel_multiplier=-1).then_inc(consts, 1)
            pool.iota(first8_i[:], pattern=[[-1, E]], base=E, channel_multiplier=0).then_inc(consts, 1)
            pool.iota(rank8_i[:], pattern=[[C, E]], base=0, channel_multiplier=0).then_inc(consts, 1)
            pool.wait_ge(wseq_in, 16)
            pool.wait_ge(a_in, 48)
            half = H // 2
            for i in range(4):
                if i >= 2:
                    pool.wait_ge(wa_ready, i - 1)
                src = wseq_sb[:, :, (i // 2) * (D // 2):(i // 2 + 1) * (D // 2)]
                for d in range(DK):
                    ins = pool.tensor_tensor(w_times_a[:, i % 2, d, :].rearrange("p (h c) -> p h c", c=DH),
                                             src[:, d, :].rearrange("p (h c) -> p h c", c=DH),
                                             a_bc[:, i % 2, :].unsqueeze(1).broadcast_to([P, half, DH]), ALU.mult)
                ins.then_inc(wa_products, 1)
            pool.wait_ge(rows_in, 16 * T)
            pool.iota(rows[:].bitcast(I32)[:, :, D + 1], pattern=[[P, T]], base=0, channel_multiplier=1).then_inc(token_number, 1)
            pool.wait_ge(token_number, 1)
            pool.wait_ge(slots_ready, 1)
            for t in range(T):
                pool.indirect_dma_start(slots_dram, bass.IndirectOffsetOnAxis(slot_i[:, t:t + 1], 0), rows[:, t, :], None,
                                        bounds_check=E * C - 1, oob_is_err=False).then_inc(scattered, 16)
            pool.wait_ge(x1_out, 16 * T)
            for e in range(E):
                for c in range(CT):
                    n = e * CT + c
                    pool.wait_ge(y_ready, n + 1)
                    pool.indirect_dma_start(out, bass.IndirectOffsetOnAxis(slot_rows[n % (2 * CT)][:].bitcast(U32)[:, D + 1:D + 2], 0),
                                            y[c][:], None, bounds_check=N - 1, oob_is_err=False).then_inc(y_out[c], 16)
            for c in range(CT):
                pool.wait_ge(y_out[c], 16 * E)

        @block.scalar
        def _(act):
            def prepare(t, k):
                if live(t, 0, T):
                    wait(act, adj_turned1, t - 1)
                    act.wait_ge(adj_loaded[k], (t // 2 + 1) * 16 if isinstance(t, int) else (t - k) * 8 + 16)
                    act.activation(adj_b[k][:], adj_in[k][:], ACT.Copy, accum_out=deg[:, k:k + 1]).then_inc(deg_ready, 1)
                if live(t, 1, T):
                    q = 1 - k
                    act.wait_ge(xn_turned, t)
                    wait(act, seq_product, t - 2)
                    act.activation(xnT[q][:].rearrange("p a b -> p (a b)"), ps[:, q, :], ACT.Copy).then_inc(xnT_ready, 1)
                    act.wait_ge(adj_turned0, t)
                    act.activation(adjT[:, 0:T // 2, bass.ds((t - 1) * P, P)],
                                   ps[:, 4, :].bitcast(BF16).rearrange("p (j i) -> p j i", i=P), ACT.Copy).then_inc(adjT_half0, 1)
            in_pairs(act, T, 2, T + 1, prepare)

            act.wait_ge(var_ready, 1)
            act.activation(newton[1][:], newton[0][:], ACT.Sqrt).then_inc(dev_ready, 1)
            act.wait_ge(args_ready, 1)
            act.activation(sumB[2][:], sumB[0][:], ACT.Exp).then_inc(exps_ready, 1)
            act.activation(sumB[3][:], sumB[0][:], ACT.Exp, scale=ALPHA).then_inc(exps_ready, 1)
            act.wait_ge(args_ready, 3)
            act.activation(AA[:, :, :, 0], sumB[4][:], ACT.Exp, scale=1.0 - ALPHA).then_inc(exps_ready, 1)
            act.activation(AA[:, :, :, 1], sumB[5][:], ACT.Exp, scale=ALPHA - 1.0).then_inc(exps_ready, 1)

            def evacuate_low(h):
                wait(act, head_done, h)
                for half in range(2):
                    act.wait_ge(head_summed, h * 2 + half + 1)
                    s = slice(half * T // 2, (half + 1) * T // 2)
                    act.activation(both[:, s, :], node_ps[:, s, VC:2 * VC], ACT.Copy, scale=1.0 / LO).then_inc(lo_ready, 1)

            def head(h, k):
                for n, j in enumerate(ACT_TILES):
                    if n == 0:
                        act.wait_ge(a_row_in[k], (h // 2 + 1) * 16 if isinstance(h, int) else (h - k) * 8 + 16)
                        act.wait_ge(value_ready, h + 1)
                    wait_apart(act, mask_ready, (h if n >= NT else h - 1) * T + ACT_TILES[n - NT] + 1)
                    act.activation(relus[n % NT][:], a_row[k][:], ACT.Relu, scale=STEEP, bias=steep_now[:, k, j:j + 1],
                                   saturate=False).then_inc(relu_ready, 1)
                    if n == 1 and live(h, 1, H):
                        evacuate_low(h - 1)
            head(0, 0)
            with act.Fori(0, (H - 2) // 2) as i:
                head(i * 2 + 1, 1)
                head(i * 2 + 2, 0)
            head(H - 1, 1)
            evacuate_low(H - 1)

            def post(t, k):
                if live(t, 2, T):
                    act.wait_ge(z_ready, t - 1)
                    wait(act, xn2_ready, t - 3)
                    act.activation(ez[k][:], z[k][:], ACT.Exp).then_inc(ez_ready, 1)
                if live(t, 0, T):
                    act.wait_ge(heads_turned, t + 1)
                    wait(act, proj_product, t - 1)
                    act.activation(headsT[k][:].rearrange("p a b -> p (a b)"), ps[:, k, :], ACT.Copy).then_inc(headsT_ready, 1)
                if live(t, 3, T):
                    q = 1 - k
                    act.wait_ge(xn2_turned, t - 2)
                    wait(act, logit_product, t - 4)
                    act.activation(xn2T[q][:].rearrange("p a b -> p (a b)"), ps[:, 4 + q, :], ACT.Copy).then_inc(xn2T_ready, 1)
            in_pairs(act, T, 6, T + 5, post)

            act.wait_ge(var_ready, 2)
            act.activation(newton[1][:], newton[0][:], ACT.Sqrt).then_inc(dev_ready, 1)
            act.wait_ge(top_gap, 1)
            act.activation(rt[1][:], rt[0][:], ACT.Exp).then_inc(top_exp, 1)

            def turn_slots(e, k):
                for c in range(CT):
                    act.wait_ge(sx_turned, e * CT + c + 1)
                    act.activation(xT[k][:, :, c * P:(c + 1) * P],
                                   ps[:, 6 + c, :].rearrange("p (a b) -> p a b", b=P), ACT.Copy).then_inc(xT_ready, 1)

            def expert(e, k, more):
                for g in range(FT // 2):
                    act.wait_ge(h_product, e * (FT // 2) + g + 1)
                    if g == 0:
                        wait(act, y_product, e * CT)
                    act.activation(hT[:, 2 * g:2 * g + 2, :].rearrange("p a b -> p (a b)"), ps[:, g % 4, :],
                                   ACT.Gelu_apprx_tanh).then_inc(h_ready, 1)
                if more:
                    turn_slots(e + 1, 1 - k)
            turn_slots(0, 0)
            expert(0, 0, True)
            expert(1, 1, True)
            with act.Fori(1, E // 2 - 1) as i:
                expert(i * 2, 0, True)
                expert(i * 2 + 1, 1, True)
            expert(E - 2, 0, True)
            expert(E - 1, 1, False)

        @block.vector
        def _(dve):
            steps = Steps(dve, dve_step)

            def copy(dst, src):
                return dve.tensor_scalar(dst, src, 1.0, None, ALU.mult)

            def center(dst, src, k, t, all_stats, ready):
                st = stats[:, k, :]
                steps.done(dve.bn_stats(st, src))
                steps.done(dve.tensor_scalar(mean[:, k:k + 1], st[:, 1:2], st[:, 4:5], 0.5, ALU.add, ALU.mult))
                copy(all_stats[:, bass.ds(t, 1), :].rearrange("p o c -> p (o c)"), st)
                dve.tensor_scalar(dst, src, mean[:, k:k + 1], None, ALU.subtract).then_inc(ready, 1)

            def inverse_deviation(st, nth):
                a, b = newton[0], newton[1]
                steps.done(dve.tensor_tensor(a[:], st[:, :, 2], st[:, :, 5], ALU.add))
                steps.done(dve.tensor_scalar(a[:], a[:], 1.0 / D, EPS, ALU.mult, ALU.add))
                steps.done(dve.tensor_tensor(b[:], st[:, :, 1], st[:, :, 4], ALU.subtract))
                steps.done(dve.tensor_tensor(b[:], b[:], b[:], ALU.mult))
                dve.scalar_tensor_tensor(out=a[:], in0=b[:], scalar=0.25, in1=a[:], op0=ALU.mult, op1=ALU.add).then_inc(var_ready, 1)
                dve.wait_ge(dev_ready, nth)
                steps.done(dve.reciprocal(rstd[:], newton[1][:]))
                steps.done(dve.tensor_tensor(newton[1][:], rstd[:], rstd[:], ALU.mult))
                steps.done(dve.scalar_tensor_tensor(out=newton[1][:], in0=newton[1][:], scalar=-0.5, in1=newton[0][:], op0=ALU.mult, op1=ALU.mult))
                steps.done(dve.scalar_tensor_tensor(out=rstd[:], in0=newton[1][:], scalar=1.5, in1=rstd[:], op0=ALU.add, op1=ALU.mult))

            def sum_w_times_a():
                for i in range(4):
                    dve.wait_ge(wa_products, i + 1)
                    for d in range(DK):
                        ins = dve.tensor_reduce(w_score[:, d, (i % 2) * H + (i // 2) * (H // 2):(i % 2) * H + (i // 2 + 1) * (H // 2)],
                                                w_times_a[:, i % 2, d, :].rearrange("p (h c) -> p h c", c=DH), AX.X, ALU.add)
                    ins.then_inc(wa_ready, 1)

            def prepare(t, k):
                if live(t, 2, T):
                    dve.wait_ge(seq_product, t - 1)
                    copy(seq[:, bass.ds(t - 2, 1), :].rearrange("p o d -> p (o d)"), ps[:, 2 + k, :])
                    copy(scores[:, bass.ds(t - 2, 1), :].rearrange("p o d -> p (o d)"), ps[:, 6, 0:2 * H]).then_inc(seq_ready, 1)
                if live(t, 0, T):
                    dve.wait_ge(x_loaded[k], (t // 2 + 1) * 16 if isinstance(t, int) else (t - k) * 8 + 16)
                    wait(dve, xn_turned, t - 1)
                    center(xn[k][:], x_in[k][:], k, t, tile_stats, xn_ready)
                    dve.wait_ge(deg_ready, t + 1)
                    steps.done(dve.tensor_scalar(lonely[:, k:k + 1], deg[:, k:k + 1], 0.0, None, ALU.is_equal))
                    dve.tensor_scalar(adj_b[k][:], adj_b[k][:], lonely[:, k:k + 1], EDGE, ALU.add, ALU.mult).then_inc(adjb_ready, 1)
                if live(t, 1, T):
                    dve.wait_ge(adj_turned1, t)
                    copy(adjT[:, T // 2:T, bass.ds((t - 1) * P, P)],
                                    ps[:, 5, :].bitcast(BF16).rearrange("p (j i) -> p j i", i=P)).then_inc(adjT_half1, 1)
                if isinstance(t, int) and t == 0:
                    sum_w_times_a()
            in_pairs(dve, T, 2, T + 2, prepare, steps, 3)

            inverse_deviation(tile_stats, 1)
            dve.wait_ge(seq_ready, T)
            steps.done(dve.tensor_tensor(scores[:], scores[:], rstd[:].unsqueeze(2).broadcast_to([P, T, 2 * H]), ALU.mult))
            dve.tensor_reduce(bmax[:], scores[:, :, H:2 * H].rearrange("p t h -> p h t"), AX.X, ALU.max).then_inc(bmax_ready, 1)
            for g in range(4):
                dve.wait_ge(s1_turned, g + 1)
                dve.tensor_copy(s1T[:, g * 512:(g + 1) * 512], ps[0:H, g, :]).then_inc(s1T_ready, 1)
            dve.wait_ge(bmax_turned, 1)
            steps.done(dve.tensor_reduce(bmaxT[:], ps[0:H, 4, 0:P], AX.X, ALU.max))
            dve.tensor_scalar(bdiag[:], ident[0:H, 0:H], bmaxT[:, 0:1], None, ALU.mult).then_inc(bdiag_ready, 1)
            dve.wait_ge(bmax_spread, 1)
            steps.done(dve.tensor_copy(B_bc[:], ps[:, 5, 0:H]))
            B_all = B_bc[:].unsqueeze(2).broadcast_to([P, H, T])
            s1 = scores[:, :, 0:H].rearrange("p t h -> p h t")
            s2 = scores[:, :, H:2 * H].rearrange("p t h -> p h t")
            dve.tensor_tensor(sumB[0][:], s2, B_all, ALU.subtract).then_inc(args_ready, 1)
            steps.done(dve.tensor_tensor(sumB[1][:], s1, B_all, ALU.add))
            dve.tensor_scalar(sumB[4][:], sumB[1][:], 0.0, None, ALU.min).then_inc(args_ready, 1)
            dve.tensor_scalar(sumB[5][:], sumB[1][:], 0.0, None, ALU.max).then_inc(args_ready, 1)
            dve.tensor_scalar(neg_b[:], s2, -1.0, None, ALU.mult)
            dve.tensor_scalar(steep_b[:], s2, STEEP, None, ALU.mult).then_inc(factors_ready, 1)
            dve.wait_ge(exps_ready, 2)
            dve.tensor_scalar(uu[:, :, :, 0], sumB[2][:], SHIFT * LO, None, ALU.mult)
            steps.done(dve.tensor_scalar(uu[:, :, :, 1], sumB[3][:], -SHIFT * LO, None, ALU.mult))
            steps.done(dve.tensor_tensor(uuV[:], uu[:], rstd[:].unsqueeze(1).unsqueeze(3).broadcast_to([P, H, T, 2]), ALU.mult))

            def values(h, k):
                dve.tensor_scalar(steep_now[:, k, :], steep_b[:, bass.ds(h, 1), :].rearrange("p o t -> p (o t)"), 1.0, None, ALU.mult)
                v = value[:].rearrange("p t (b c) -> p t b c", b=2)
                u, uV = (a[:, bass.ds(h, 1), :, :].rearrange("p o t b -> p (o t) b") for a in (uu, uuV))
                dve.tensor_tensor(v[:, :, :, 0:DH], seq[:, :, bass.ds(h * DH, DH)].unsqueeze(2).broadcast_to([P, T, 2, DH]),
                                  uV.unsqueeze(3).broadcast_to([P, T, 2, DH]), ALU.mult)
                dve.tensor_copy(v[:, :, :, DH], u).then_inc(value_ready, 1)

            def split(h, k):
                dve.wait_ge(value_ready, h + 1)
                tb = tables[k]
                steps.done(dve.tensor_scalar(tb[:, :, 0:VC], value[:], 1.0 / LO, None, ALU.mult))
                steps.done(dve.scalar_tensor_tensor(out=tb[:, :, VC:2 * VC], in0=tb[:, :, 0:VC], scalar=-LO, in1=value[:],
                                                    op0=ALU.mult, op1=ALU.add))
                dve.tensor_scalar(tb[:, :, 2 * VC:3 * VC].rearrange("p t (b c) -> p t b c", b=2),
                                  tb[:, :, 0:2 * VC].rearrange("p t (b c) -> p t b c", b=2)[:, :, :, DC:VC],
                                  -1.0, None, ALU.mult).then_inc(table_ready, 1)

            def combine(h):
                for half in range(2):
                    s = slice(half * T // 2, (half + 1) * T // 2)
                    dve.wait_ge(lo_ready, h * 2 + half + 1)
                    ins = dve.tensor_tensor(both[:, s, :], node_ps[:, s, 0:VC], both[:, s, :], ALU.add).then_inc(sums_free, 1)
                dve.wait_ge(sums_free, h * 2 + 4)
                b4 = both[:].rearrange("p t (b c) -> p t b c", b=2)
                A = AA[:, bass.ds(h, 1), :, :].rearrange("p o t b -> p (o t) b").unsqueeze(3).broadcast_to([P, T, 2, DC])
                steps.done(dve.tensor_tensor(b4, b4, A, ALU.mult))
                dve.tensor_tensor(hid[:, :, bass.ds(h, 1), :].rearrange("p t o c -> p t (o c)"), b4[:, :, 0, :], b4[:, :, 1, :],
                                  ALU.add).then_inc(head_done, 1)

            dve.sem_inc(sums_free, 2)
            dve.wait_ge(slot_init_out, 16)
            values(0, 0)
            split(0, 0)
            dve.wait_ge(factors_ready, 1)
            dve.wait_ge(adjT_half0, T)
            dve.wait_ge(adjT_half1, T)
            dve.wait_ge(exps_ready, 4)
            dve.wait_ge(s1T_out, 16)

            def head(h, k):
                def compare(d):
                    j = DVE_TILES[d]
                    dve.tensor_scalar(above[d % 2][:], a_row[k][:], neg_b[:, bass.ds(h, 1), j:j + 1].rearrange("p o q -> p (o q)"),
                                      EDGE, ALU.is_gt, ALU.mult).then_inc(above_ready, 1)

                dve.wait_ge(a_row_in[k], (h // 2 + 1) * 16 if isinstance(h, int) else (h - k) * 8 + 16)
                compare(0)
                r = d = 0
                for j in range(T):
                    if j < NM:
                        wait(dve, mask_used, h * T + j + 1 - NM)
                    else:
                        dve.wait_ge(mask_used, h * T + j + 1 - NM)
                    if j in DVE_TILES:
                        dve.wait_ge(above_ready, h * len(DVE_TILES) + d + 1)
                        source, d = above[d % 2], d + 1
                    else:
                        dve.wait_ge(relu_ready, h * len(ACT_TILES) + r + 1)
                        source, r = relus[r % NT], r + 1
                    dve.tensor_tensor(masks[j % NM][:].bitcast(I32), source[:].bitcast(I32), adjT[:, j, :].bitcast(I32),
                                      ALU.bitwise_and).then_inc(mask_ready, 1)
                    if j in DVE_TILES and d < len(DVE_TILES):
                        compare(d)
                    if j == 2 and live(h, 1, H):
                        combine(h - 1)
                    if not isinstance(h, int) or h + 1 < H:
                        if j == 6:
                            values(h + 1, 1 - k)
                        if j == 12:
                            split(h + 1, 1 - k)
            head(0, 0)
            per = 3
            start = steps.base + steps.n
            with dve.Fori(0, (H - 2) // 2) as i:
                for k in range(2):
                    steps.base, steps.n = start + i * (2 * per) + k * per, 0
                    head(i * 2 + (1 + k), 1 - k)
                    assert steps.n == per
            steps.base, steps.n = start + (H - 2) * per, 0
            head(H - 1, 1)
            combine(H - 1)

            dve.wait_ge(head_done, H)
            dve.wait_ge(post_in, 32)
            dve.wait_ge(rows_in, 16 * T)

            def post(t, k):
                if live(t, 5, T):
                    q = 1 - k
                    dve.wait_ge(logit_product, t - 4)
                    copy(logits[:, bass.ds(t - 5, 1), :].rearrange("p o e -> p (o e)"), ps[:, 6 + q, 0:E]).then_inc(logits_ready, 1)
                if live(t, 0, T):
                    hd = hid[:, bass.ds(t, 1), :, :].rearrange("p o h c -> p (o h) c")
                    steps.done(dve.reciprocal(rden[:, k, :], hd[:, :, DH]))
                    wait(dve, heads_turned, t - 1)
                    dve.tensor_tensor(heads[k][:].rearrange("p (h c) -> p h c", c=DH), hd[:, :, 0:DH],
                                      rden[:, k, :].unsqueeze(2).broadcast_to([P, H, DH]), ALU.mult).then_inc(heads_ready, 1)
                if live(t, 2, T):
                    dve.wait_ge(proj_product, t - 1)
                    dve.tensor_tensor(z[k][:], ps[:, 2 + k, :], bout_bc[:], ALU.add).then_inc(z_ready, 1)
                if live(t, 3, T):
                    q = 1 - k
                    row = rows[:, bass.ds(t - 3, 1), 0:D].rearrange("p o d -> p (o d)")
                    dve.wait_ge(ez_ready, t - 2)
                    steps.done(dve.tensor_scalar(ez[q][:], ez[q][:], 1.0, -1.0, ALU.min, ALU.add))
                    steps.done(dve.scalar_tensor_tensor(out=ez[q][:], in0=z[q][:], scalar=0.0, in1=ez[q][:], op0=ALU.max, op1=ALU.add))
                    steps.done(dve.tensor_tensor(ez[q][:], row, ez[q][:], ALU.add))
                    copy(row, ez[q][:])
                    wait(dve, xn2_turned, t - 4)
                    center(xn2[q][:], ez[q][:], q, t - 3, tile_stats, xn2_ready)
            in_pairs(dve, T, 6, T + 5, post, steps, 6)

            dve.wait_ge(logits_ready, T)
            dve.wait_ge(heads_turned, T)
            dve.wait_ge(consts, 8)
            inverse_deviation(tile_stats, 2)
            steps.done(dve.tensor_tensor(newton[0][:], tile_stats[:, :, 1], tile_stats[:, :, 4], ALU.add))
            dve.tensor_scalar(rows[:, :, D + 2], newton[0][:], 0.5, None, ALU.mult)
            dve.tensor_copy(rows[:, :, D + 3], rstd[:])
            steps.done(dve.tensor_tensor(logits[:], logits[:], rstd[:].unsqueeze(2).broadcast_to([P, T, E]), ALU.mult))
            top = rt1[0]
            steps.done(dve.tensor_reduce(top[:], logits[:], AX.X, ALU.max))
            top_all = top[:].unsqueeze(2).broadcast_to([P, T, E])
            dve.tensor_tensor(rt[0][:], logits[:], top_all, ALU.subtract).then_inc(top_gap, 1)
            dve.tensor_copy(first8[:], first8_i[:])
            dve.tensor_copy(rank8[:], rank8_i[:])
            steps.done(dve.tensor_tensor(rt[2][:], logits[:], top_all, ALU.is_equal))
            steps.done(dve.tensor_tensor(rt[2][:], rt[2][:], first8[:].unsqueeze(1).broadcast_to([P, T, E]), ALU.mult))
            steps.done(dve.tensor_reduce(rt1[1][:], rt[2][:], AX.X, ALU.max))
            steps.done(dve.tensor_tensor(rt[3][:], rt[2][:], rt1[1][:].unsqueeze(2).broadcast_to([P, T, E]), ALU.is_equal))
            steps.done(dve.tensor_copy(oh_b[:], rt[3][:]))
            steps.done(dve.memset(rt[4][:], 0.0))
            steps.done(dve.tensor_copy(rt[4][:, 1:T, :], rt[3][:, 0:T - 1, :]))
            a, b, d = rt[4], rt[5], 1
            while d < T:
                dve.tensor_copy(b[:, 0:d, :], a[:, 0:d, :])
                steps.done(dve.tensor_tensor(b[:, d:T, :], a[:, d:T, :], a[:, 0:T - d, :], ALU.add))
                a, b, d = b, a, 2 * d
            dve.tensor_copy(cum_b[:], a[:]).then_inc(onehot_ready, 1)
            dve.wait_ge(top_exp, 1)
            steps.done(dve.tensor_reduce(rt1[2][:], rt[1][:], AX.X, ALU.add))
            dve.reciprocal(rows[:, :, D], rt1[2][:])
            steps.done(dve.tensor_tensor(rt[6][:], rt[3][:], rank8[:].unsqueeze(1).broadcast_to([P, T, E]), ALU.mult))
            steps.done(dve.tensor_reduce(rt1[3][:], rt[6][:], AX.X, ALU.add))
            dve.wait_ge(counts_ready, 1)
            steps.done(dve.tensor_tensor(rt[7][:], ps[:, 0, 0:T * E].rearrange("p (t e) -> p t e", e=E), rt[3][:], ALU.mult))
            steps.done(dve.tensor_reduce(rt1[4][:], rt[7][:], AX.X, ALU.add))
            steps.done(dve.tensor_scalar(rt1[5][:], rt1[4][:], float(C), float(OFF), ALU.is_ge, ALU.mult))
            steps.done(dve.tensor_tensor(rt1[4][:], rt1[4][:], rt1[5][:], ALU.add))
            steps.done(dve.tensor_tensor(rt1[4][:], rt1[4][:], rt1[3][:], ALU.add))
            dve.tensor_copy(slot_i[:], rt1[4][:]).then_inc(slots_ready, 1)

            def norm_slots(e, k):
                dve.wait_ge(slot_in[k], (e // 2 + 1) * 16 * CT if isinstance(e, int) else (e - k) * 8 * CT + 16 * CT)
                for c in range(CT):
                    wait(dve, sx_turned, (e - 1) * CT + c + 1)
                    r = slot_rows[CT * k + c]
                    dve.tensor_scalar(slot_xn[c][:], r[:, 0:D], r[:, D + 2:D + 3], r[:, D + 3:D + 4], ALU.subtract, ALU.mult).then_inc(sx_ready, 1)

            def expert(e, k, more):
                if more:
                    norm_slots(e + 1, 1 - k)
                for c in range(CT):
                    dve.wait_ge(y_product, e * CT + c + 1)
                    wait(dve, y_out[c], e * 16)
                    r = slot_rows[CT * k + c]
                    dve.scalar_tensor_tensor(out=y[c][:], in0=ps[:, 4 + c, :], scalar=r[:, D:D + 1], in1=r[:, 0:D],
                                             op0=ALU.mult, op1=ALU.add).then_inc(y_ready, 1)
            norm_slots(0, 0)
            expert(0, 0, True)
            expert(1, 1, True)
            with dve.Fori(1, E // 2 - 1) as i:
                expert(i * 2, 0, True)
                expert(i * 2 + 1, 1, True)
            expert(E - 2, 0, True)
            expert(E - 1, 1, False)

        @block.tensor
        def _(pe):
            pe.wait_ge(consts, 8)
            pe.wait_ge(wseq_in, 16)

            def turn(dst_bank, src, ready):
                for d in range(DK):
                    ins = pe.transpose(ps[:, dst_bank, d * P:(d + 1) * P], src[:, d * P:(d + 1) * P], ident[:])
                ins.then_inc(ready, 1)

            def prepare(t, k):
                if live(t, 1, T):
                    q = 1 - k
                    pe.wait_ge(xnT_ready, t)
                    wait(pe, seq_ready, t - 2)
                    for d in range(DK):
                        pe.matmul(ps[:, 2 + q, :], xnT[q][:, d, :], wseq_sb[:, d, :], start=(d == 0), stop=(d == DK - 1))
                    if isinstance(t, int) and t == 1:
                        pe.wait_ge(wa_ready, 4)
                    wait(pe, seq_ready, t - 1)
                    for d in range(DK):
                        ins = pe.matmul(ps[:, 6, 0:2 * H], xnT[q][:, d, :], w_score[:, d, :], start=(d == 0), stop=(d == DK - 1))
                    ins.then_inc(seq_product, 1)
                if live(t, 0, T):
                    pe.wait_ge(xn_ready, t + 1)
                    wait(pe, xnT_ready, t - 1)
                    turn(k, xn[k], xn_turned)
                    pe.wait_ge(adjb_ready, t + 1)
                    for half, (left, turned) in enumerate(((adjT_half0, adj_turned0), (adjT_half1, adj_turned1))):
                        wait(pe, left, t)
                        bank = ps[:, 4 + half, :].bitcast(BF16)
                        for j in range(T // 2):
                            jt = half * (T // 2) + j
                            ins = pe.transpose(bank[:, j * P:(j + 1) * P], adj_b[k][:, jt * P:(jt + 1) * P], ident_b[:])
                        ins.then_inc(turned, 1)
            in_pairs(pe, T, 2, T + 1, prepare)

            pe.wait_ge(seq_ready, T)
            pe.wait_ge(adjT_half0, T)
            pe.wait_ge(adjT_half1, T)
            pe.wait_ge(bmax_ready, 1)
            for g in range(4):
                for t in range(4 * g, 4 * g + 4):
                    ins = pe.transpose(ps[0:H, g, (t % 4) * P:(t % 4 + 1) * P], scores[:, t, 0:H], ident[:])
                ins.then_inc(s1_turned, 1)
            pe.transpose(ps[0:H, 4, 0:P], bmax[:], ident[:]).then_inc(bmax_turned, 1)
            pe.wait_ge(bdiag_ready, 1)
            pe.matmul(ps[:, 5, 0:H], ones[:], bdiag[:], start=True, stop=True).then_inc(bmax_spread, 1)
            pe.wait_ge(s1T_ready, 4)
            pe.wait_ge(value_ready, 1)

            with pe.Fori(0, H // 2) as i:
                for k in range(2):
                    h = i * 2 + k
                    wait_apart(pe, table_ready, h + 1)
                    tb = tables[k]
                    for j in range(T):
                        wait_apart(pe, mask_ready, h * T + j + 1)
                        for n in range(T):
                            if j == 0 and n % (T // 2) == 0:
                                wait_apart(pe, sums_free, h * 2 + 1 + n // (T // 2))
                            cols = slice(n * P, (n + 1) * P)
                            ins = pe.matmul(node_ps[:, n, 0:2 * VC], masks[j % NM][:, cols].bitcast(F8), tb[:, j, 0:2 * VC],
                                            start=(j == 0 and n % 2 == 0), stop=False, skip_group_check=True)
                            if n == T - 1:
                                ins.then_inc(mask_used, 1)
                            ins = pe.matmul(node_ps[:, n, 0:2 * VC].rearrange("p (b c) -> p b c", b=2)[:, :, DC:VC],
                                            adjT[:, j, cols].bitcast(F8), tb[:, j, 2 * VC:3 * VC].rearrange("p (b c) -> p b c", b=2),
                                            start=False, stop=(j == T - 1), skip_group_check=True)
                            if j == T - 1 and (n + 1) % (T // 2) == 0:
                                ins.then_inc(head_summed, 1)

            pe.wait_ge(post_in, 32)
            pe.wait_ge(sums_free, 2 * H + 2)

            def post(t, k):
                q = 1 - k
                if live(t, 1, T):
                    pe.wait_ge(headsT_ready, t)
                    wait(pe, z_ready, t - 2)
                    for d in range(DK):
                        ins = pe.matmul(ps[:, 2 + q, :], headsT[q][:, d, :], wout_sb[:, d, :], start=(d == 0), stop=(d == DK - 1))
                    ins.then_inc(proj_product, 1)
                if live(t, 4, T):
                    pe.wait_ge(xn2T_ready, t - 3)
                    wait(pe, logits_ready, t - 5)
                    for d in range(DK):
                        ins = pe.matmul(ps[:, 6 + k, 0:E], xn2T[k][:, d, :], router_sb[:, d, :], start=(d == 0), stop=(d == DK - 1))
                    ins.then_inc(logit_product, 1)
                if live(t, 0, T):
                    pe.wait_ge(heads_ready, t + 1)
                    wait(pe, headsT_ready, t - 1)
                    turn(k, heads[k], heads_turned)
                if live(t, 3, T):
                    pe.wait_ge(xn2_ready, t - 2)
                    wait(pe, xn2T_ready, t - 4)
                    turn(4 + q, xn2[q], xn2_turned)
            in_pairs(pe, T, 6, T + 5, post)

            pe.wait_ge(onehot_ready, 1)
            counts = ps[:, 0, 0:T * E]
            pe.matmul(counts, earlier_b[:], oh_b[:].rearrange("p t e -> p (t e)"), start=True, stop=False)
            pe.matmul(counts, ones_b[:], cum_b[:].rearrange("p t e -> p (t e)"), start=False, stop=True).then_inc(counts_ready, 1)

            def turn_slots(e):
                for c in range(CT):
                    pe.wait_ge(sx_ready, e * CT + c + 1)
                    wait(pe, xT_ready, (e - 1) * CT + c + 1)
                    turn(6 + c, slot_xn[c], sx_turned)

            def expert(e, k, more):
                pe.wait_ge(w_in[0][k], (e // 2 + 1) * 16 if isinstance(e, int) else (e - k) * 8 + 16)
                pe.wait_ge(xT_ready, e * CT + CT)
                for g in range(FT // 2):
                    wait(pe, h_ready, e * (FT // 2) + g - 3)
                    for f in range(2 * g, 2 * g + 2):
                        for d in range(DK):
                            ins = pe.matmul(ps[:, g % 4, (f % 2) * C:(f % 2 + 1) * C], w1_sb[k][:, d, f * P:(f + 1) * P], xT[k][:, d, :],
                                            start=(f % 2 == 0 and d == 0), stop=(d == DK - 1), skip_group_check=True)
                    ins.then_inc(h_product, 1)
                if more:
                    turn_slots(e + 1)
                pe.wait_ge(w_in[1][k], (e // 2 + 1) * 16 if isinstance(e, int) else (e - k) * 8 + 16)
                for c in range(CT):
                    wait(pe, y_ready, (e - 1) * CT + c + 1)
                    for f in range(FT):
                        pe.wait_ge(h_ready, e * (FT // 2) + f // 2 + 1)
                        ins = pe.matmul(ps[:, 4 + c, :], hT[:, f, c * P:(c + 1) * P], w2_sb[k][:, f, :], start=(f == 0), stop=(f == FT - 1))
                    ins.then_inc(y_product, 1)
            pe.wait_ge(slots_ready, 1)
            turn_slots(0)
            expert(0, 0, True)
            expert(1, 1, True)
            with pe.Fori(1, E // 2 - 1) as i:
                expert(i * 2, 0, True)
                expert(i * 2 + 1, 1, True)
            expert(E - 2, 0, True)
            expert(E - 1, 1, False)


_INS = ["x", "adj", "L0_gnn_W_seq", "L0_gnn_a1", "L0_gnn_a2", "L0_gnn_W_out", "L0_gnn_b_out",
        "L0_ffn_router_w", "L0_ffn_w1", "L0_ffn_w2"]


def kernel(**inputs):
    import numpy as _np
    import concourse.bacc as _bacc
    from concourse import mybir as _mybir
    from concourse.bass_utils import run_bass_kernel_spmd as _run

    nc = _bacc.Bacc("TRN2", target_bir_lowering=False, num_devices=1)
    arrays, args = {}, []
    for name in _INS:
        a = _np.ascontiguousarray(inputs[name])
        arrays[f"in_{name}_dram"] = a
        args.append(nc.dram_tensor(f"in_{name}_dram", a.shape, _mybir.dt.from_np(a.dtype), kind="ExternalInput").ap())
    out = nc.dram_tensor("out_0_dram", inputs["x"].shape, _mybir.dt.float32, kind="ExternalOutput").ap()
    gnn_moe(nc, *args, out)
    r = _run(nc, [arrays], core_ids=[0])
    return r.results[0]["out_0_dram"]
```

```python
from contextlib import ExitStack

import concourse.bass as bass
from concourse import mybir

ALU = mybir.AluOpType
ACT = mybir.ActivationFunctionType
AX = mybir.AxisListType
F32 = mybir.dt.float32
BF16 = mybir.dt.bfloat16
F16 = mybir.dt.float16
I32 = mybir.dt.int32
U8 = mybir.dt.uint8
F8 = mybir.dt.float8e4
U32 = mybir.dt.uint32
F32R = mybir.dt.float32r

P = 128
EPS = 1e-5
ALPHA = 0.2
LO = 2048.0
SHIFT = 256.0
STEEP = 2.0 ** 100
EDGE = 112.0
OFF = 4096
DVE_TILES = (2, 5, 8, 11, 14)


def live(t, back, tiles):
    return not isinstance(t, int) or 0 <= t - back < tiles


def wait(eng, sem, count):
    if not isinstance(count, int) or count > 0:
        eng.wait_ge(sem, count)


class Steps:

    def __init__(self, eng, sem):
        self.eng, self.sem, self.base, self.n = eng, sem, 0, 0

    def done(self, ins):
        ins.then_inc(self.sem, 1)
        self.n += 1
        self.eng.wait_ge(self.sem, self.base + self.n)


def in_pairs(eng, tiles, first, last, body, steps=None, per=0):
    for t in range(first):
        body(t, t % 2)
    loops = (tiles - first) // 2
    if steps:
        start, steps.n, before = steps.base, 0, steps.n
        start = start + before
    with eng.Fori(0, loops) as i:
        for k in range(2):
            if steps:
                steps.base, steps.n = start + i * (2 * per) + k * per, 0
            body(i * 2 + (first + k), k)
            assert not steps or steps.n == per, (steps.n, per)
    if steps:
        steps.base, steps.n = start + loops * 2 * per, 0
    for t in range(tiles, last):
        body(t, t % 2)


def gnn_moe(nc, x, adj, W_seq, a1, a2, W_out, b_out, router_w, w1, w2, out):
    N, D = x.shape
    DH = a1.shape[0]
    H = D // DH
    E, _, F = w1.shape
    C = N // E
    T = N // P
    DK = D // P
    FT = F // P
    CT = C // P
    GP = FT // 2
    WC = 4
    FC = FT // WC
    DC = DH + 1
    VC = 2 * DC
    ROW = D + 4
    ACT_TILES = [j for j in range(T) if j not in DVE_TILES]
    ROW_LOADS = 4
    NT, NM = 11, 8
    assert len(ACT_TILES) % NT == 0 and T % NM == 0

    s1T_dram = nc.dram_tensor("s1T_dram", (H, N), F32, kind="Internal").ap()
    slots_dram = nc.dram_tensor("slots_dram", (E * C, ROW), F32, kind="Internal").ap()

    with ExitStack() as ctx:
        def sem(name):
            return ctx.enter_context(nc.semaphore(name))

        CONST = 14336
        SIZE = 212608
        arena = ctx.enter_context(nc.sbuf_tensor("arena", [P, SIZE // 4], F32))
        cursor = [0]
        start_of = {}

        def at(offset, name, shape, dt):
            size = {F32: 4, F32R: 4, I32: 4, U32: 4, BF16: 2, F16: 2, U8: 1, F8: 1}[dt]
            n = size
            for s in shape[1:]:
                n *= s
            start_of[name] = offset
            cursor[0] = offset + (n + 31) // 32 * 32
            assert cursor[0] <= SIZE, (name, cursor[0])
            return nc.alloc_sbuf_tensor_at(name, shape, dt, offset=ARENA + offset)

        def after(name, shape, dt):
            return at(cursor[0], name, shape, dt)

        ARENA = 16512

        ident = at(0, "ident", [P, P], F32)
        ident_b = after("ident_b", [P, P], BF16)
        ones = after("ones", [H, P], F32)
        ones_b = after("ones_b", [P, P], BF16)
        earlier_b = after("earlier_b", [P, P], BF16)
        a_bc = after("a_bc", [P, 2, DH], F32)
        scores = after("scores", [P, T, 2 * H], F32)
        uu = after("uu", [P, H, T, 2], F32)
        uuV = after("uuV", [P, H, T, 2], F32)
        AA = after("AA", [P, H, T, 2], F32)
        neg_b = after("neg_b", [P, H, T], F32)
        steep_b = after("steep_b", [P, H, T], F32)
        steep_now = after("steep_now", [P, 2, T], F32)
        bmax = after("bmax", [P, H], F32)
        bmaxT = after("bmaxT", [H, 1], F32)
        bdiag = after("bdiag", [H, H], F32)
        B_bc = after("B_bc", [P, H], F32)
        stats = after("stats", [P, 2, 6], F32)
        mean = after("mean", [P, 2], F32)
        tile_stats = after("tile_stats", [P, T, 6], F32)
        rstd = after("rstd", [P, T], F32)
        newton = [after(f"newton{k}", [P, T], F32) for k in range(2)]
        deg = after("deg", [P, 2], F32)
        lonely = after("lonely", [P, 2], F32)
        router_sb = after("router_sb", [P, DK, E], F32)
        rden = after("rden", [P, 2, H], F32)
        logits = after("logits", [P, T, E], F32)
        rank8 = after("rank8", [P, E], F32)
        first8 = after("first8", [P, E], F32)
        rank8_i = after("rank8_i", [P, E], I32)
        first8_i = after("first8_i", [P, E], I32)
        slot_i = after("slot_i", [P, T], U32)
        assert cursor[0] <= CONST, cursor[0]

        wout_sb = at(CONST, "wout_sb", [P, DK, D], F32)
        bout_bc = after("bout_bc", [P, D], F32)
        MAIN = cursor[0]

        adjT = at(MAIN, "adjT", [P, T, N], U8)
        above = [after(f"above{k}", [P, N], U8) for k in range(len(DVE_TILES))]
        relus = [after(f"relu{k}", [P, N], F8) for k in range(NT)]
        hid = after("hid", [P, T, H, DC], F32)
        tables = [after(f"tables{k}", [P, T, 3 * VC], F16) for k in range(2)]
        value = after("value", [P, T, VC], F32)
        both = after("both", [P, T, VC], F32)
        seq = after("seq", [P, T, D], F32)
        a_row = [after(f"a_row{k}", [P, N], F32) for k in range(2)]
        a_row_end = cursor[0]
        masks = [at(SIZE - (NM - k) * N, f"mask{k}", [P, N], U8) for k in range(NM)]
        assert a_row_end <= start_of["mask0"]

        adj_in = [at(start_of["hid"], "adj_in0", [P, N], F32), after("adj_in1", [P, N], F32)]
        adj_b = [after(f"adj_b{k}", [P, N], BF16) for k in range(2)]
        x_in = [after(f"x_in{k}", [P, D], F32) for k in range(2)]
        xn = [after(f"xn{k}", [P, D], F32) for k in range(2)]
        assert cursor[0] <= start_of["tables0"] 
        slot_init = at(start_of["tables0"], "slot_init", [P, ROW], F32)
        w_times_a = after("w_times_a", [P, 2, DK, D // 2], F32)
        assert cursor[0] <= start_of["seq"]
        wseq_sb = at(start_of["a_row0"], "wseq_sb", [P, DK, D], F32)
        xnT = [after(f"xnT{k}", [P, DK, P], F32) for k in range(2)]
        w_score = after("w_score", [P, DK, 2 * H], F32)
        assert cursor[0] <= start_of["mask0"]
        s1T = at(start_of["mask0"], "s1T", [H, N], F32)
        sumB = [after(f"sumB{k}", [P, H, T], F32) for k in range(6)]

        rows = at(MAIN, "rows", [P, T, ROW], F32)
        heads = [after(f"heads{k}", [P, D], F32) for k in range(2)]
        headsT = [after(f"headsT{k}", [P, DK, P], F32) for k in range(2)]
        z = [after(f"z{k}", [P, D], F32) for k in range(2)]
        xn2 = [after(f"xn2_{k}", [P, D], F32) for k in range(2)]
        xn2T = [after(f"xn2T{k}", [P, DK, P], F32) for k in range(2)]
        assert cursor[0] <= start_of["hid"], (cursor[0], start_of["hid"])

        def parts(offset, name, shape):
            raw = at(offset, f"{name}_raw", shape, F32)
            lo = at(offset, f"{name}_lo", shape, F32R)
            return raw, after(f"{name}_hi", shape, F32R), lo

        W_BASE = SIZE - 2 * WC * 2 * FC * D * 4
        w2_raw, w2_hi, w2_lo = zip(*(parts(W_BASE + c * 2 * FC * D * 4, f"w2_{c}", [P, FC, D]) for c in range(WC)))
        w1_raw, w1_hi, w1_lo = zip(*(parts(W_BASE + (WC + c) * 2 * FC * D * 4, f"w1_{c}", [P, DK, F // WC]) for c in range(WC)))
        xT_hi = [at(CONST, "xT_hi0", [P, DK, C], F32R), after("xT_hi1", [P, DK, C], F32R)]
        xT_lo = [after(f"xT_lo{k}", [P, DK, C], F32R) for k in range(2)]
        h_raw, h_hi, h_lo = parts(cursor[0], "h", [P, FT, C])
        slot_rows = [after("slot_rows0", [P, ROW], F32)]
        slot_rows += [after(f"slot_rows{k}", [P, ROW], F32) for k in range(1, 2 * CT)]
        slot_xn = [after(f"slot_xn{k}", [P, D], F32) for k in range(CT)]
        y = [after(f"y{k}", [P, D], F32) for k in range(CT)]
        assert cursor[0] <= W_BASE, (cursor[0], W_BASE)
        ez = [at(start_of["scores"], "ez0", [P, D], F32), at(start_of["uu"], "ez1", [P, D], F32)]
        rt = [at(start_of["heads0"] + 512 * k, f"rt{k}", [P, T, E], F32) for k in range(8)]
        rt1 = [at(start_of["heads0"] + 4096 + 64 * k, f"rt1_{k}", [P, T], F32) for k in range(6)]
        cum_b = at(start_of["heads0"] + 4608, "cum_b", [P, T, E], BF16)
        oh_b = at(start_of["heads0"] + 4864, "oh_b", [P, T, E], BF16)

        ps = ctx.enter_context(nc.psum_tensor("ps", [P, 8, 512], F32))
        node_ps = ps[:, :, :].rearrange("p b (i c) -> p (b i) c", i=2)

        pool_step, dve_step = sem("pool_step"), sem("dve_step")
        consts = sem("consts")
        wseq_in, a_in, slot_init_out = sem("wseq_in"), sem("a_in"), sem("slot_init_out")
        x_loaded = [sem(f"x_loaded{k}") for k in range(2)]
        adj_loaded = [sem(f"adj_loaded{k}") for k in range(2)]
        wa_products, wa_ready = sem("wa_products"), sem("wa_ready")
        xn_ready, deg_ready, adjb_ready = sem("xn_ready"), sem("deg_ready"), sem("adjb_ready")
        xn_turned, adj_turned0, adj_turned1 = sem("xn_turned"), sem("adj_turned0"), sem("adj_turned1")
        xnT_ready, adjT_half0, adjT_half1 = sem("xnT_ready"), sem("adjT_half0"), sem("adjT_half1")
        seq_product, seq_ready = sem("seq_product"), sem("seq_ready")
        s1_turned, s1T_ready, s1T_out = sem("s1_turned"), sem("s1T_ready"), sem("s1T_out")
        bmax_ready, bmax_turned = sem("bmax_ready"), sem("bmax_turned")
        bdiag_ready, bmax_spread = sem("bdiag_ready"), sem("bmax_spread")
        var_ready, dev_ready = sem("var_ready"), sem("dev_ready")
        args_ready, exps_ready, factors_ready = sem("args_ready"), sem("exps_ready"), sem("factors_ready")
        a_row_in = [sem(f"a_row_in{k}") for k in range(2)]
        relu_ready, above_ready = sem("relu_ready"), sem("above_ready")
        mask_ready, mask_used = sem("mask_ready"), sem("mask_used")
        value_ready, table_ready = sem("value_ready"), sem("table_ready")
        head_summed, lo_ready, sums_free = sem("head_summed"), sem("lo_ready"), sem("sums_free")
        head_done = sem("head_done")
        post_in, rows_in = sem("post_in"), sem("rows_in")
        heads_ready, heads_turned, headsT_ready = sem("heads_ready"), sem("heads_turned"), sem("headsT_ready")
        proj_product, z_ready, ez_ready = sem("proj_product"), sem("z_ready"), sem("ez_ready")
        mean_ready, row_ready = sem("mean_ready"), sem("row_ready")
        xn2_ready, xn2_turned, xn2T_ready = sem("xn2_ready"), sem("xn2_turned"), sem("xn2T_ready")
        logit_product, logits_ready, x1_out = sem("logit_product"), sem("logits_ready"), sem("x1_out")
        top_gap, top_exp, onehot_ready = sem("top_gap"), sem("top_exp"), sem("onehot_ready")
        counts_ready, slots_ready, scattered = sem("counts_ready"), sem("slots_ready"), sem("scattered")
        token_number = sem("token_number")
        waited = sem("waited")
        w1_in, w2_in = ([sem(f"w{m}_in{c}") for c in range(WC)] for m in (1, 2))
        w_hi_ready, w_ready, w2_used = sem("w_hi_ready"), sem("w_ready"), sem("w2_used")
        xT_hi_ready, h_hi_ready = sem("xT_hi_ready"), sem("h_hi_ready")
        slot_in = [sem(f"slot_in{k}") for k in range(2)]
        sx_ready, sx_turned, xT_ready = sem("sx_ready"), sem("sx_turned"), sem("xT_ready")
        h_product, h_ready, y_product, y_ready = sem("h_product"), sem("h_ready"), sem("y_product"), sem("y_ready")
        y_out = [sem(f"y_out{c}") for c in range(CT)]

        def wait_apart(eng, sem, count):
            wait(eng, sem, count)
            if not isinstance(count, int):
                eng.sem_inc(waited, 1)

        block = ctx.enter_context(nc.Block())

        @block.sync
        def _(sp):
            sp.dma_start(wseq_sb[:], W_seq.rearrange("(k p) n -> p k n", p=P)).then_inc(wseq_in, 16)
            for i, a in enumerate((a1, a2)):
                sp.dma_start(a_bc[:, i, :], a.rearrange("(o d) -> o d", o=1).broadcast_to([P, DH])).then_inc(a_in, 16)
            sp.dma_start(router_sb[:], router_w.rearrange("(k p) e -> p k e", p=P)).then_inc(a_in, 16)

            def load(t, k):
                wait(sp, xn_ready, t - 1)
                sp.dma_start(x_in[k][:], x[bass.ds(t * P, P), :]).then_inc(x_loaded[k], 16)
                wait(sp, deg_ready, t - 1)
                sp.dma_start(adj_in[k][:], adj[bass.ds(t * P, P), :]).then_inc(adj_loaded[k], 16)
            in_pairs(sp, T, 2, T, load)

            sp.wait_ge(consts, 8)
            sp.dma_start(slots_dram.rearrange("(n p) r -> p n r", p=P),
                         slot_init[:].unsqueeze(1).broadcast_to([P, T, ROW])).then_inc(slot_init_out, 16)
            sp.wait_ge(s1T_ready, 4)
            sp.dma_start(s1T_dram, s1T[:]).then_inc(s1T_out, 16)
            sp.wait_ge(s1T_out, 16)
            sp.wait_ge(slot_init_out, 16)
            sp.wait_ge(seq_ready, T)

            def load_a(h, k):
                wait(sp, mask_ready, (h - 1) * T)
                sp.dma_start(a_row[k][:], s1T_dram[bass.ds(h, 1), :].broadcast_to([P, N])).then_inc(a_row_in[k], 16)
            in_pairs(sp, H, 2, H, load_a)
            sp.dma_start(wout_sb[:], W_out.rearrange("(k p) n -> p k n", p=P)).then_inc(post_in, 16)
            sp.dma_start(bout_bc[:], b_out.rearrange("(o d) -> o d", o=1).broadcast_to([P, D])).then_inc(post_in, 16)

            sp.wait_ge(head_summed, 2 * H)
            sp.wait_ge(head_done, H)
            for q in range(ROW_LOADS):
                n = T // ROW_LOADS
                sp.dma_start(rows[:, q * n:(q + 1) * n, 0:D],
                             x[q * n * P:(q + 1) * n * P, :].rearrange("(t p) d -> p t d", p=P)).then_inc(rows_in, 16)

            def load_w1(e, c):
                sp.dma_start(w1_raw[c][:], w1[bass.ds(e, 1), :, c * (F // WC):(c + 1) * (F // WC)]
                             .rearrange("o (k p) f -> p (o k) f", p=P)).then_inc(w1_in[c], 16)

            def load_w2(e, c):
                sp.dma_start(w2_raw[c][:], w2[bass.ds(e, 1), c * FC * P:(c + 1) * FC * P, :]
                             .rearrange("o (k p) d -> p (o k) d", p=P)).then_inc(w2_in[c], 16)
            for c in range(WC):
                load_w1(0, c)
            load_w2(0, WC - 1)

            def store(t, k):
                sp.wait_ge(row_ready, t + 1)
                sp.dma_start(out[bass.ds(t * P, P), :], rows[:, bass.ds(t, 1), 0:D].rearrange("p o d -> p (o d)")).then_inc(x1_out, 16)
            in_pairs(sp, T, 2, T, store)
            sp.wait_ge(heads_ready, T)
            for c in range(WC - 1):
                load_w2(0, c)

            def load_slots(e, k):
                for c in range(CT):
                    wait(sp, y_out[c], 16 * (e - 1))
                for c in range(CT):
                    sp.dma_start(slot_rows[CT * k + c][:], slots_dram[bass.ds(e * C + c * P, P), :]).then_inc(slot_in[k], 16)
            sp.wait_ge(scattered, 16 * T)
            load_slots(0, 0)
            load_slots(1, 1)

            def refill(e, k, more=True):
                for c in range(WC):
                    sp.wait_ge(h_product, (e - 1) * GP + (c + 1) * (GP // WC))
                    load_w1(e, c)
                for c in range(WC):
                    if c < WC - 1:
                        sp.wait_ge(w2_used, (e - 1) * (WC - 1) + c + 1)
                    else:
                        sp.wait_ge(y_product, e * CT)
                    load_w2(e, c)
                if more:
                    load_slots(e + 1, 1 - k)
            refill(1, 1)
            with sp.Fori(1, E // 2 - 1) as i:
                refill(i * 2, 0)
                refill(i * 2 + 1, 1)
            refill(E - 2, 0)
            refill(E - 1, 1, more=False)
            sp.wait_ge(x1_out, 16 * T)

        @block.gpsimd
        def _(pool):
            pool.memset(ident[:], 0.0).then_inc(pool_step, 1)
            pool.memset(ones_b[:], 1.0).then_inc(consts, 1)
            pool.memset(ones[:], 1.0).then_inc(consts, 1)
            pool.memset(slot_init[:], 0.0).then_inc(pool_step, 1)
            pool.wait_ge(pool_step, 2)
            pool.affine_select(out=ident[:], in_=ident[:], compare_op=ALU.not_equal, fill=1.0, base=0,
                               pattern=[[-1, P]], channel_multiplier=1).then_inc(consts, 1)
            pool.memset(slot_init[:].bitcast(I32)[:, D + 1:D + 2], OFF).then_inc(consts, 1)
            pool.wait_ge(consts, 3)
            pool.tensor_copy(ident_b[:], ident[:]).then_inc(consts, 1)
            pool.affine_select(out=earlier_b[:], in_=ones_b[:], compare_op=ALU.is_gt, fill=0.0, base=0,
                               pattern=[[1, P]], channel_multiplier=-1).then_inc(consts, 1)
            pool.iota(first8_i[:], pattern=[[-1, E]], base=E, channel_multiplier=0).then_inc(consts, 1)
            pool.iota(rank8_i[:], pattern=[[C, E]], base=0, channel_multiplier=0).then_inc(consts, 1)
            pool.wait_ge(wseq_in, 16)
            pool.wait_ge(a_in, 48)
            half = H // 2
            for i in range(4):
                if i >= 2:
                    pool.wait_ge(wa_ready, i - 1)
                src = wseq_sb[:, :, (i // 2) * (D // 2):(i // 2 + 1) * (D // 2)]
                for d in range(DK):
                    ins = pool.tensor_tensor(w_times_a[:, i % 2, d, :].rearrange("p (h c) -> p h c", c=DH),
                                             src[:, d, :].rearrange("p (h c) -> p h c", c=DH),
                                             a_bc[:, i % 2, :].unsqueeze(1).broadcast_to([P, half, DH]), ALU.mult)
                ins.then_inc(wa_products, 1)
            pool.wait_ge(rows_in, 16 * ROW_LOADS)
            pool.iota(rows[:].bitcast(I32)[:, :, D + 1], pattern=[[P, T]], base=0, channel_multiplier=1).then_inc(token_number, 1)
            pool.wait_ge(token_number, 1)
            pool.wait_ge(slots_ready, 1)
            pool.wait_ge(row_ready, T)
            for t in range(T):
                pool.indirect_dma_start(slots_dram, bass.IndirectOffsetOnAxis(slot_i[:, t:t + 1], 0), rows[:, t, :], None,
                                        bounds_check=E * C - 1, oob_is_err=False).then_inc(scattered, 16)
            pool.wait_ge(x1_out, 16 * T)
            for e in range(E):
                for c in range(CT):
                    n = e * CT + c
                    pool.wait_ge(y_ready, n + 1)
                    pool.indirect_dma_start(out, bass.IndirectOffsetOnAxis(slot_rows[n % (2 * CT)][:].bitcast(U32)[:, D + 1:D + 2], 0),
                                            y[c][:], None, bounds_check=N - 1, oob_is_err=False).then_inc(y_out[c], 16)
            for c in range(CT):
                pool.wait_ge(y_out[c], 16 * E)

        @block.scalar
        def _(act):
            def prepare(t, k):
                if live(t, 0, T):
                    wait(act, adj_turned1, t - 1)
                    act.wait_ge(adj_loaded[k], (t // 2 + 1) * 16 if isinstance(t, int) else (t - k) * 8 + 16)
                    act.activation(adj_b[k][:], adj_in[k][:], ACT.Copy, accum_out=deg[:, k:k + 1]).then_inc(deg_ready, 1)
                if live(t, 1, T):
                    q = 1 - k
                    act.wait_ge(xn_turned, t)
                    wait(act, seq_product, t - 2)
                    act.activation(xnT[q][:].rearrange("p a b -> p (a b)"), ps[:, q, :], ACT.Copy).then_inc(xnT_ready, 1)
                    act.wait_ge(adj_turned0, t)
                    act.activation(adjT[:, 0:T // 2, bass.ds((t - 1) * P, P)],
                                   ps[:, 4, :].bitcast(BF16).rearrange("p (j i) -> p j i", i=P), ACT.Copy).then_inc(adjT_half0, 1)
            in_pairs(act, T, 2, T + 1, prepare)

            act.wait_ge(var_ready, 1)
            act.activation(newton[1][:], newton[0][:], ACT.Sqrt).then_inc(dev_ready, 1)
            for g in range(4):
                act.wait_ge(s1_turned, g + 1)
                act.activation(s1T[:, g * 512:(g + 1) * 512], ps[0:H, g, :], ACT.Copy).then_inc(s1T_ready, 1)
            act.wait_ge(args_ready, 1)
            act.activation(sumB[2][:], sumB[0][:], ACT.Exp).then_inc(exps_ready, 1)
            act.activation(sumB[3][:], sumB[0][:], ACT.Exp, scale=ALPHA).then_inc(exps_ready, 1)
            act.wait_ge(args_ready, 3)
            act.activation(AA[:, :, :, 0], sumB[4][:], ACT.Exp, scale=1.0 - ALPHA).then_inc(exps_ready, 1)
            act.activation(AA[:, :, :, 1], sumB[5][:], ACT.Exp, scale=ALPHA - 1.0).then_inc(exps_ready, 1)

            def evacuate_low(h):
                wait(act, head_done, h)
                for half in range(2):
                    act.wait_ge(head_summed, h * 2 + half + 1)
                    s = slice(half * T // 2, (half + 1) * T // 2)
                    act.activation(both[:, s, :], node_ps[:, s, VC:2 * VC], ACT.Copy, scale=1.0 / LO).then_inc(lo_ready, 1)

            def head(h, k):
                for n, j in enumerate(ACT_TILES):
                    if n == 0:
                        act.wait_ge(a_row_in[k], (h // 2 + 1) * 16 if isinstance(h, int) else (h - k) * 8 + 16)
                        act.wait_ge(value_ready, h + 1)
                    wait_apart(act, mask_ready, (h if n >= NT else h - 1) * T + ACT_TILES[n - NT] + 1)
                    act.activation(relus[n % NT][:], a_row[k][:], ACT.Relu, scale=STEEP, bias=steep_now[:, k, j:j + 1],
                                   saturate=False).then_inc(relu_ready, 1)
                    if n == 3 and live(h, 1, H):
                        evacuate_low(h - 1)
            head(0, 0)
            with act.Fori(0, (H - 2) // 2) as i:
                head(i * 2 + 1, 1)
                head(i * 2 + 2, 0)
            head(H - 1, 1)
            evacuate_low(H - 1)

            def post(t, k):
                q = 1 - k
                if live(t, 0, T):
                    act.wait_ge(heads_turned, t + 1)
                    wait(act, proj_product, t - 1)
                    act.activation(headsT[k][:].rearrange("p a b -> p (a b)"), ps[:, k, :], ACT.Copy).then_inc(headsT_ready, 1)
                if live(t, 5, T):
                    act.wait_ge(xn2_turned, t - 4)
                    wait(act, logit_product, t - 6)
                    act.activation(xn2T[q][:].rearrange("p a b -> p (a b)"), ps[:, 4 + q, :], ACT.Copy).then_inc(xn2T_ready, 1)
                if live(t, 3, T):
                    act.wait_ge(z_ready, t - 2)
                    wait(act, row_ready, t - 4)
                    act.activation(ez[q][:], z[q][:], ACT.Exp).then_inc(ez_ready, 1)
                if live(t, 4, T):
                    act.wait_ge(mean_ready, t - 3)
                    wait(act, xn2_turned, t - 5)
                    act.activation(xn2[k][:], ez[k][:], ACT.Identity, bias=mean[:, k:k + 1]).then_inc(xn2_ready, 1)
                    act.activation(rows[:, bass.ds(t - 4, 1), 0:D].rearrange("p o d -> p (o d)"), ez[k][:], ACT.Copy).then_inc(row_ready, 1)
            in_pairs(act, T, 8, T + 7, post)

            act.wait_ge(var_ready, 2)
            act.activation(newton[1][:], newton[0][:], ACT.Sqrt).then_inc(dev_ready, 1)
            act.wait_ge(top_gap, 1)
            act.activation(rt[1][:], rt[0][:], ACT.Exp).then_inc(top_exp, 1)

            def turn_slots(e, k):
                for c in range(CT):
                    act.wait_ge(sx_turned, e * CT + c + 1)
                    act.activation(xT_hi[k][:, :, c * P:(c + 1) * P],
                                   ps[:, 6 + c, :].rearrange("p (a b) -> p a b", b=P), ACT.Copy).then_inc(xT_hi_ready, 1)

            def first_part(hi, raw, loaded, e):
                act.wait_ge(loaded, e * 16 + 16)
                act.activation(hi[:], raw[:], ACT.Copy).then_inc(w_hi_ready, 1)

            def expert(e, k, more):
                for g in range(GP):
                    act.wait_ge(h_product, e * GP + g + 1)
                    for dst in (h_raw, h_hi):
                        ins = act.activation(dst[:, 2 * g:2 * g + 2, :].rearrange("p a b -> p (a b)"), ps[:, g % 4, :], ACT.Gelu_apprx_tanh)
                    ins.then_inc(h_hi_ready, 1)
                    if g % 2 == 0:
                        first_part(w2_hi[g // 2], w2_raw[g // 2], w2_in[g // 2], e)
                if more:
                    turn_slots(e + 1, 1 - k)
                    for c in range(WC):
                        first_part(w1_hi[c], w1_raw[c], w1_in[c], e + 1)
            for c in range(WC):
                first_part(w1_hi[c], w1_raw[c], w1_in[c], 0)
            turn_slots(0, 0)
            expert(0, 0, True)
            expert(1, 1, True)
            with act.Fori(1, E // 2 - 1) as i:
                expert(i * 2, 0, True)
                expert(i * 2 + 1, 1, True)
            expert(E - 2, 0, True)
            expert(E - 1, 1, False)

        @block.vector
        def _(dve):
            steps = Steps(dve, dve_step)

            def copy(dst, src):
                return dve.tensor_scalar(dst, src, 1.0, None, ALU.mult)

            def center(dst, src, k, t, all_stats, ready):
                st = stats[:, k, :]
                steps.done(dve.bn_stats(st, src))
                steps.done(dve.tensor_scalar(mean[:, k:k + 1], st[:, 1:2], st[:, 4:5], 0.5, ALU.add, ALU.mult))
                copy(all_stats[:, bass.ds(t, 1), :].rearrange("p o c -> p (o c)"), st)
                dve.tensor_scalar(dst, src, mean[:, k:k + 1], None, ALU.subtract).then_inc(ready, 1)

            def inverse_deviation(st, nth):
                a, b = newton[0], newton[1]
                steps.done(dve.tensor_tensor(a[:], st[:, :, 2], st[:, :, 5], ALU.add))
                steps.done(dve.tensor_scalar(a[:], a[:], 1.0 / D, EPS, ALU.mult, ALU.add))
                steps.done(dve.tensor_tensor(b[:], st[:, :, 1], st[:, :, 4], ALU.subtract))
                steps.done(dve.tensor_tensor(b[:], b[:], b[:], ALU.mult))
                dve.scalar_tensor_tensor(out=a[:], in0=b[:], scalar=0.25, in1=a[:], op0=ALU.mult, op1=ALU.add).then_inc(var_ready, 1)
                dve.wait_ge(dev_ready, nth)
                steps.done(dve.reciprocal(rstd[:], newton[1][:]))
                steps.done(dve.tensor_tensor(newton[1][:], rstd[:], rstd[:], ALU.mult))
                steps.done(dve.scalar_tensor_tensor(out=newton[1][:], in0=newton[1][:], scalar=-0.5, in1=newton[0][:], op0=ALU.mult, op1=ALU.mult))
                steps.done(dve.scalar_tensor_tensor(out=rstd[:], in0=newton[1][:], scalar=1.5, in1=rstd[:], op0=ALU.add, op1=ALU.mult))

            def sum_w_times_a():
                for i in range(4):
                    dve.wait_ge(wa_products, i + 1)
                    for d in range(DK):
                        ins = dve.tensor_reduce(w_score[:, d, (i % 2) * H + (i // 2) * (H // 2):(i % 2) * H + (i // 2 + 1) * (H // 2)],
                                                w_times_a[:, i % 2, d, :].rearrange("p (h c) -> p h c", c=DH), AX.X, ALU.add)
                    ins.then_inc(wa_ready, 1)

            def prepare(t, k):
                if live(t, 2, T):
                    dve.wait_ge(seq_product, t - 1)
                    copy(seq[:, bass.ds(t - 2, 1), :].rearrange("p o d -> p (o d)"), ps[:, 2 + k, :])
                    copy(scores[:, bass.ds(t - 2, 1), :].rearrange("p o d -> p (o d)"), ps[:, 6, 0:2 * H]).then_inc(seq_ready, 1)
                if live(t, 0, T):
                    dve.wait_ge(x_loaded[k], (t // 2 + 1) * 16 if isinstance(t, int) else (t - k) * 8 + 16)
                    wait(dve, xn_turned, t - 1)
                    center(xn[k][:], x_in[k][:], k, t, tile_stats, xn_ready)
                    dve.wait_ge(deg_ready, t + 1)
                    steps.done(dve.tensor_scalar(lonely[:, k:k + 1], deg[:, k:k + 1], 0.0, None, ALU.is_equal))
                    dve.tensor_scalar(adj_b[k][:], adj_b[k][:], lonely[:, k:k + 1], EDGE, ALU.add, ALU.mult).then_inc(adjb_ready, 1)
                if live(t, 1, T):
                    dve.wait_ge(adj_turned1, t)
                    copy(adjT[:, T // 2:T, bass.ds((t - 1) * P, P)],
                                    ps[:, 5, :].bitcast(BF16).rearrange("p (j i) -> p j i", i=P)).then_inc(adjT_half1, 1)
                if isinstance(t, int) and t == 0:
                    sum_w_times_a()
            in_pairs(dve, T, 2, T + 2, prepare, steps, 3)

            inverse_deviation(tile_stats, 1)
            dve.wait_ge(seq_ready, T)
            steps.done(dve.tensor_tensor(scores[:], scores[:], rstd[:].unsqueeze(2).broadcast_to([P, T, 2 * H]), ALU.mult))
            dve.tensor_reduce(bmax[:], scores[:, :, H:2 * H].rearrange("p t h -> p h t"), AX.X, ALU.max).then_inc(bmax_ready, 1)
            dve.wait_ge(bmax_turned, 1)
            steps.done(dve.tensor_reduce(bmaxT[:], ps[0:H, 4, 0:P], AX.X, ALU.max))
            dve.tensor_scalar(bdiag[:], ident[0:H, 0:H], bmaxT[:, 0:1], None, ALU.mult).then_inc(bdiag_ready, 1)
            dve.wait_ge(bmax_spread, 1)
            steps.done(dve.tensor_copy(B_bc[:], ps[:, 5, 0:H]))
            B_all = B_bc[:].unsqueeze(2).broadcast_to([P, H, T])
            s1 = scores[:, :, 0:H].rearrange("p t h -> p h t")
            s2 = scores[:, :, H:2 * H].rearrange("p t h -> p h t")
            dve.tensor_tensor(sumB[0][:], s2, B_all, ALU.subtract).then_inc(args_ready, 1)
            steps.done(dve.tensor_tensor(sumB[1][:], s1, B_all, ALU.add))
            dve.tensor_scalar(sumB[4][:], sumB[1][:], 0.0, None, ALU.min).then_inc(args_ready, 1)
            dve.tensor_scalar(sumB[5][:], sumB[1][:], 0.0, None, ALU.max).then_inc(args_ready, 1)
            dve.tensor_scalar(neg_b[:], s2, -1.0, None, ALU.mult)
            dve.tensor_scalar(steep_b[:], s2, STEEP, None, ALU.mult).then_inc(factors_ready, 1)
            dve.wait_ge(exps_ready, 2)
            dve.tensor_scalar(uu[:, :, :, 0], sumB[2][:], SHIFT * LO, None, ALU.mult)
            steps.done(dve.tensor_scalar(uu[:, :, :, 1], sumB[3][:], -SHIFT * LO, None, ALU.mult))
            steps.done(dve.tensor_tensor(uuV[:], uu[:], rstd[:].unsqueeze(1).unsqueeze(3).broadcast_to([P, H, T, 2]), ALU.mult))

            def values(h, k):
                dve.tensor_scalar(steep_now[:, k, :], steep_b[:, bass.ds(h, 1), :].rearrange("p o t -> p (o t)"), 1.0, None, ALU.mult)
                v = value[:].rearrange("p t (b c) -> p t b c", b=2)
                u, uV = (a[:, bass.ds(h, 1), :, :].rearrange("p o t b -> p (o t) b") for a in (uu, uuV))
                dve.tensor_tensor(v[:, :, :, 0:DH], seq[:, :, bass.ds(h * DH, DH)].unsqueeze(2).broadcast_to([P, T, 2, DH]),
                                  uV.unsqueeze(3).broadcast_to([P, T, 2, DH]), ALU.mult)
                dve.tensor_copy(v[:, :, :, DH], u).then_inc(value_ready, 1)

            def split(h, k):
                dve.wait_ge(value_ready, h + 1)
                tb = tables[k]
                steps.done(dve.tensor_scalar(tb[:, :, 0:VC], value[:], 1.0 / LO, None, ALU.mult))
                steps.done(dve.scalar_tensor_tensor(out=tb[:, :, VC:2 * VC], in0=tb[:, :, 0:VC], scalar=-LO, in1=value[:],
                                                    op0=ALU.mult, op1=ALU.add))
                dve.tensor_scalar(tb[:, :, 2 * VC:3 * VC].rearrange("p t (b c) -> p t b c", b=2),
                                  tb[:, :, 0:2 * VC].rearrange("p t (b c) -> p t b c", b=2)[:, :, :, DC:VC],
                                  -1.0, None, ALU.mult).then_inc(table_ready, 1)

            def combine(h):
                for half in range(2):
                    s = slice(half * T // 2, (half + 1) * T // 2)
                    dve.wait_ge(lo_ready, h * 2 + half + 1)
                    ins = dve.tensor_tensor(both[:, s, :], node_ps[:, s, 0:VC], both[:, s, :], ALU.add).then_inc(sums_free, 1)

            def weigh(h):
                dve.wait_ge(sums_free, h * 2 + 4)
                b4 = both[:].rearrange("p t (b c) -> p t b c", b=2)
                A = AA[:, bass.ds(h, 1), :, :].rearrange("p o t b -> p (o t) b").unsqueeze(3).broadcast_to([P, T, 2, DC])
                steps.done(dve.tensor_tensor(b4, b4, A, ALU.mult))
                dve.tensor_tensor(hid[:, :, bass.ds(h, 1), :].rearrange("p t o c -> p t (o c)"), b4[:, :, 0, :], b4[:, :, 1, :],
                                  ALU.add).then_inc(head_done, 1)

            dve.sem_inc(sums_free, 2)
            dve.wait_ge(slot_init_out, 16)
            values(0, 0)
            split(0, 0)
            dve.wait_ge(factors_ready, 1)
            dve.wait_ge(adjT_half0, T)
            dve.wait_ge(adjT_half1, T)
            dve.wait_ge(exps_ready, 4)
            dve.wait_ge(s1T_out, 16)

            def head(h, k):
                def compare(d):
                    j = DVE_TILES[d]
                    dve.tensor_scalar(above[d][:], a_row[k][:], neg_b[:, bass.ds(h, 1), j:j + 1].rearrange("p o q -> p (o q)"),
                                      EDGE, ALU.is_gt, ALU.mult).then_inc(above_ready, 1)

                dve.wait_ge(a_row_in[k], (h // 2 + 1) * 16 if isinstance(h, int) else (h - k) * 8 + 16)
                compare(0)
                r = d = 0
                for j in range(T):
                    if j < NM:
                        wait(dve, mask_used, h * T + j + 1 - NM)
                    else:
                        dve.wait_ge(mask_used, h * T + j + 1 - NM)
                    if j in DVE_TILES:
                        dve.wait_ge(above_ready, h * len(DVE_TILES) + d + 1)
                        source, d = above[d], d + 1
                    else:
                        dve.wait_ge(relu_ready, h * len(ACT_TILES) + r + 1)
                        source, r = relus[r % NT], r + 1
                    dve.tensor_tensor(masks[j % NM][:].bitcast(I32), source[:].bitcast(I32), adjT[:, j, :].bitcast(I32),
                                      ALU.bitwise_and).then_inc(mask_ready, 1)
                    if j == 3 and live(h, 1, H):
                        combine(h - 1)
                    if j == 7 and live(h, 1, H):
                        weigh(h - 1)
                    if j in DVE_TILES and d < len(DVE_TILES):
                        compare(d)
                    if not isinstance(h, int) or h + 1 < H:
                        if j == 9:
                            values(h + 1, 1 - k)
                        if j == 12:
                            split(h + 1, 1 - k)
            head(0, 0)
            per = 3
            start = steps.base + steps.n
            with dve.Fori(0, (H - 2) // 2) as i:
                for k in range(2):
                    steps.base, steps.n = start + i * (2 * per) + k * per, 0
                    head(i * 2 + (1 + k), 1 - k)
                    assert steps.n == per
            steps.base, steps.n = start + (H - 2) * per, 0
            head(H - 1, 1)
            combine(H - 1)
            weigh(H - 1)

            dve.wait_ge(head_done, H)
            dve.wait_ge(post_in, 32)

            def post(t, k):
                q = 1 - k
                if live(t, 7, T):
                    dve.wait_ge(logit_product, t - 6)
                    copy(logits[:, bass.ds(t - 7, 1), :].rearrange("p o e -> p (o e)"), ps[:, 6 + q, 0:E]).then_inc(logits_ready, 1)
                if live(t, 0, T):
                    hd = hid[:, bass.ds(t, 1), :, :].rearrange("p o h c -> p (o h) c")
                    steps.done(dve.reciprocal(rden[:, k, :], hd[:, :, DH]))
                    wait(dve, heads_turned, t - 1)
                    dve.tensor_tensor(heads[k][:].rearrange("p (h c) -> p h c", c=DH), hd[:, :, 0:DH],
                                      rden[:, k, :].unsqueeze(2).broadcast_to([P, H, DH]), ALU.mult).then_inc(heads_ready, 1)
                if live(t, 3, T):
                    dve.wait_ge(proj_product, t - 2)
                    dve.tensor_tensor(z[q][:], ps[:, 2 + q, :], bout_bc[:], ALU.add).then_inc(z_ready, 1)
                if live(t, 4, T):
                    if isinstance(t, int) and t == 4:
                        dve.wait_ge(rows_in, 16 * ROW_LOADS)
                    row = rows[:, bass.ds(t - 4, 1), 0:D].rearrange("p o d -> p (o d)")
                    dve.wait_ge(ez_ready, t - 3)
                    steps.done(dve.tensor_scalar(ez[k][:], ez[k][:], 1.0, -1.0, ALU.min, ALU.add))
                    steps.done(dve.scalar_tensor_tensor(out=ez[k][:], in0=z[k][:], scalar=0.0, in1=ez[k][:], op0=ALU.max, op1=ALU.add))
                    steps.done(dve.tensor_tensor(ez[k][:], row, ez[k][:], ALU.add))
                    st = stats[:, k, :]
                    steps.done(dve.bn_stats(st, ez[k][:]))
                    wait(dve, xn2_ready, t - 5)
                    dve.tensor_scalar(mean[:, k:k + 1], st[:, 1:2], st[:, 4:5], -0.5, ALU.add, ALU.mult).then_inc(mean_ready, 1)
                    copy(tile_stats[:, bass.ds(t - 4, 1), :].rearrange("p o c -> p (o c)"), st)
            in_pairs(dve, T, 8, T + 7, post, steps, 5)

            dve.wait_ge(logits_ready, T)
            dve.wait_ge(heads_turned, T)
            dve.wait_ge(consts, 8)
            inverse_deviation(tile_stats, 2)
            steps.done(dve.tensor_tensor(newton[0][:], tile_stats[:, :, 1], tile_stats[:, :, 4], ALU.add))
            dve.tensor_scalar(rows[:, :, D + 2], newton[0][:], 0.5, None, ALU.mult)
            dve.tensor_copy(rows[:, :, D + 3], rstd[:])
            steps.done(dve.tensor_tensor(logits[:], logits[:], rstd[:].unsqueeze(2).broadcast_to([P, T, E]), ALU.mult))
            top = rt1[0]
            steps.done(dve.tensor_reduce(top[:], logits[:], AX.X, ALU.max))
            top_all = top[:].unsqueeze(2).broadcast_to([P, T, E])
            dve.tensor_tensor(rt[0][:], logits[:], top_all, ALU.subtract).then_inc(top_gap, 1)
            dve.tensor_copy(first8[:], first8_i[:])
            dve.tensor_copy(rank8[:], rank8_i[:])
            steps.done(dve.tensor_tensor(rt[2][:], logits[:], top_all, ALU.is_equal))
            steps.done(dve.tensor_tensor(rt[2][:], rt[2][:], first8[:].unsqueeze(1).broadcast_to([P, T, E]), ALU.mult))
            steps.done(dve.tensor_reduce(rt1[1][:], rt[2][:], AX.X, ALU.max))
            steps.done(dve.tensor_tensor(rt[3][:], rt[2][:], rt1[1][:].unsqueeze(2).broadcast_to([P, T, E]), ALU.is_equal))
            steps.done(dve.tensor_copy(oh_b[:], rt[3][:]))
            steps.done(dve.memset(rt[4][:], 0.0))
            steps.done(dve.tensor_copy(rt[4][:, 1:T, :], rt[3][:, 0:T - 1, :]))
            a, b, d = rt[4], rt[5], 1
            while d < T:
                dve.tensor_copy(b[:, 0:d, :], a[:, 0:d, :])
                steps.done(dve.tensor_tensor(b[:, d:T, :], a[:, d:T, :], a[:, 0:T - d, :], ALU.add))
                a, b, d = b, a, 2 * d
            dve.tensor_copy(cum_b[:], a[:]).then_inc(onehot_ready, 1)
            dve.wait_ge(top_exp, 1)
            steps.done(dve.tensor_reduce(rt1[2][:], rt[1][:], AX.X, ALU.add))
            dve.reciprocal(rows[:, :, D], rt1[2][:])
            steps.done(dve.tensor_tensor(rt[6][:], rt[3][:], rank8[:].unsqueeze(1).broadcast_to([P, T, E]), ALU.mult))
            steps.done(dve.tensor_reduce(rt1[3][:], rt[6][:], AX.X, ALU.add))
            dve.wait_ge(counts_ready, 1)
            steps.done(dve.tensor_tensor(rt[7][:], ps[:, 0, 0:T * E].rearrange("p (t e) -> p t e", e=E), rt[3][:], ALU.mult))
            steps.done(dve.tensor_reduce(rt1[4][:], rt[7][:], AX.X, ALU.add))
            steps.done(dve.tensor_scalar(rt1[5][:], rt1[4][:], float(C), float(OFF), ALU.is_ge, ALU.mult))
            steps.done(dve.tensor_tensor(rt1[4][:], rt1[4][:], rt1[5][:], ALU.add))
            steps.done(dve.tensor_tensor(rt1[4][:], rt1[4][:], rt1[3][:], ALU.add))
            dve.tensor_copy(slot_i[:], rt1[4][:]).then_inc(slots_ready, 1)

            def norm_slots(e, k):
                dve.wait_ge(slot_in[k], (e // 2 + 1) * 16 * CT if isinstance(e, int) else (e - k) * 8 * CT + 16 * CT)
                for c in range(CT):
                    wait(dve, sx_turned, (e - 1) * CT + c + 1)
                    r = slot_rows[CT * k + c]
                    dve.tensor_scalar(slot_xn[c][:], r[:, 0:D], r[:, D + 2:D + 3], r[:, D + 3:D + 4], ALU.subtract, ALU.mult).then_inc(sx_ready, 1)

            def second_part(lo, raw, hi, count):
                dve.wait_ge(w_hi_ready, count)
                dve.tensor_tensor(lo[:], raw[:], hi[:].bitcast(F32), ALU.subtract).then_inc(w_ready, 1)

            def turn_slots(e, k):
                for c in range(CT):
                    s = slice(c * P, (c + 1) * P)
                    dve.wait_ge(xT_hi_ready, e * CT + c + 1)
                    dve.tensor_tensor(xT_lo[k][:, :, s], ps[:, 6 + c, :].rearrange("p (a b) -> p a b", b=P),
                                      xT_hi[k][:, :, s].bitcast(F32), ALU.subtract).then_inc(xT_ready, 1)

            def expert(e, k, more):
                for g in range(GP):
                    pair = slice(2 * g, 2 * g + 2)
                    dve.wait_ge(h_hi_ready, e * GP + g + 1)
                    dve.tensor_tensor(h_lo[:, pair, :], h_raw[:, pair, :], h_hi[:, pair, :].bitcast(F32), ALU.subtract).then_inc(h_ready, 1)
                    if g % 2 == 0:
                        second_part(w2_lo[g // 2], w2_raw[g // 2], w2_hi[g // 2], e * 2 * WC + WC + g // 2 + 1)
                    if g == 3 and more:
                        norm_slots(e + 1, 1 - k)
                if more:
                    turn_slots(e + 1, 1 - k)
                    for c in range(WC):
                        second_part(w1_lo[c], w1_raw[c], w1_hi[c], (e + 1) * 2 * WC + c + 1)
                for c in range(CT):
                    dve.wait_ge(y_product, e * CT + c + 1)
                    wait(dve, y_out[c], e * 16)
                    r = slot_rows[CT * k + c]
                    dve.scalar_tensor_tensor(out=y[c][:], in0=ps[:, 4 + c, :], scalar=r[:, D:D + 1], in1=r[:, 0:D],
                                             op0=ALU.mult, op1=ALU.add).then_inc(y_ready, 1)
            for c in range(WC):
                second_part(w1_lo[c], w1_raw[c], w1_hi[c], c + 1)
            norm_slots(0, 0)
            turn_slots(0, 0)
            expert(0, 0, True)
            expert(1, 1, True)
            with dve.Fori(1, E // 2 - 1) as i:
                expert(i * 2, 0, True)
                expert(i * 2 + 1, 1, True)
            expert(E - 2, 0, True)
            expert(E - 1, 1, False)

        @block.tensor
        def _(pe):
            pe.wait_ge(consts, 8)
            pe.wait_ge(wseq_in, 16)

            def turn(dst_bank, src, ready):
                for d in range(DK):
                    ins = pe.transpose(ps[:, dst_bank, d * P:(d + 1) * P], src[:, d * P:(d + 1) * P], ident[:])
                ins.then_inc(ready, 1)

            def prepare(t, k):
                if live(t, 1, T):
                    q = 1 - k
                    pe.wait_ge(xnT_ready, t)
                    wait(pe, seq_ready, t - 2)
                    for d in range(DK):
                        pe.matmul(ps[:, 2 + q, :], xnT[q][:, d, :], wseq_sb[:, d, :], start=(d == 0), stop=(d == DK - 1))
                    if isinstance(t, int) and t == 1:
                        pe.wait_ge(wa_ready, 4)
                    wait(pe, seq_ready, t - 1)
                    for d in range(DK):
                        ins = pe.matmul(ps[:, 6, 0:2 * H], xnT[q][:, d, :], w_score[:, d, :], start=(d == 0), stop=(d == DK - 1))
                    ins.then_inc(seq_product, 1)
                if live(t, 0, T):
                    pe.wait_ge(xn_ready, t + 1)
                    wait(pe, xnT_ready, t - 1)
                    turn(k, xn[k], xn_turned)
                    pe.wait_ge(adjb_ready, t + 1)
                    for half, (left, turned) in enumerate(((adjT_half0, adj_turned0), (adjT_half1, adj_turned1))):
                        wait(pe, left, t)
                        bank = ps[:, 4 + half, :].bitcast(BF16)
                        for j in range(T // 2):
                            jt = half * (T // 2) + j
                            ins = pe.transpose(bank[:, j * P:(j + 1) * P], adj_b[k][:, jt * P:(jt + 1) * P], ident_b[:])
                        ins.then_inc(turned, 1)
            in_pairs(pe, T, 2, T + 1, prepare)

            pe.wait_ge(seq_ready, T)
            pe.wait_ge(adjT_half0, T)
            pe.wait_ge(adjT_half1, T)
            pe.wait_ge(bmax_ready, 1)
            pe.transpose(ps[0:H, 4, 0:P], bmax[:], ident[:]).then_inc(bmax_turned, 1)
            for g in range(4):
                for t in range(4 * g, 4 * g + 4):
                    ins = pe.transpose(ps[0:H, g, (t % 4) * P:(t % 4 + 1) * P], scores[:, t, 0:H], ident[:])
                ins.then_inc(s1_turned, 1)
                if g == 0:
                    pe.wait_ge(bdiag_ready, 1)
                    pe.matmul(ps[:, 5, 0:H], ones[:], bdiag[:], start=True, stop=True).then_inc(bmax_spread, 1)
            pe.wait_ge(s1T_ready, 4)
            pe.wait_ge(value_ready, 1)

            with pe.Fori(0, H // 2) as i:
                for k in range(2):
                    h = i * 2 + k
                    wait_apart(pe, table_ready, h + 1)
                    tb = tables[k]
                    for half, j in ((b, a + c) for a in range(0, T, 2) for b in range(2) for c in range(2)):
                        if half == 0:
                            wait_apart(pe, mask_ready, h * T + j + 1)
                        if j == 0:
                            wait_apart(pe, sums_free, h * 2 + 1 + half)
                        for n in range(half * T // 2, (half + 1) * T // 2):
                            cols = slice(n * P, (n + 1) * P)
                            ins = pe.matmul(node_ps[:, n, 0:2 * VC], masks[j % NM][:, cols].bitcast(F8), tb[:, j, 0:2 * VC],
                                            start=(j == 0 and n % 2 == 0), stop=False, skip_group_check=True)
                            if n == T - 1:
                                ins.then_inc(mask_used, 1)
                            ins = pe.matmul(node_ps[:, n, 0:2 * VC].rearrange("p (b c) -> p b c", b=2)[:, :, DC:VC],
                                            adjT[:, j, cols].bitcast(F8), tb[:, j, 2 * VC:3 * VC].rearrange("p (b c) -> p b c", b=2),
                                            start=False, stop=(j == T - 1), skip_group_check=True)
                        if j == T - 1:
                            ins.then_inc(head_summed, 1)

            pe.wait_ge(post_in, 32)
            pe.wait_ge(sums_free, 2 * H + 2)

            def post(t, k):
                q = 1 - k
                if live(t, 2, T):
                    pe.wait_ge(headsT_ready, t - 1)
                    wait(pe, z_ready, t - 3)
                    for d in range(DK):
                        ins = pe.matmul(ps[:, 2 + k, :], headsT[k][:, d, :], wout_sb[:, d, :], start=(d == 0), stop=(d == DK - 1))
                    ins.then_inc(proj_product, 1)
                if live(t, 6, T):
                    pe.wait_ge(xn2T_ready, t - 5)
                    wait(pe, logits_ready, t - 7)
                    for d in range(DK):
                        ins = pe.matmul(ps[:, 6 + k, 0:E], xn2T[k][:, d, :], router_sb[:, d, :], start=(d == 0), stop=(d == DK - 1))
                    ins.then_inc(logit_product, 1)
                if live(t, 0, T):
                    pe.wait_ge(heads_ready, t + 1)
                    wait(pe, headsT_ready, t - 1)
                    turn(k, heads[k], heads_turned)
                if live(t, 5, T):
                    pe.wait_ge(xn2_ready, t - 4)
                    wait(pe, xn2T_ready, t - 6)
                    turn(4 + q, xn2[q], xn2_turned)
            in_pairs(pe, T, 8, T + 7, post)

            pe.wait_ge(onehot_ready, 1)
            counts = ps[:, 0, 0:T * E]
            pe.matmul(counts, earlier_b[:], oh_b[:].rearrange("p t e -> p (t e)"), start=True, stop=False)
            pe.matmul(counts, ones_b[:], cum_b[:].rearrange("p t e -> p (t e)"), start=False, stop=True).then_inc(counts_ready, 1)

            def turn_slots(e):
                for c in range(CT):
                    pe.wait_ge(sx_ready, e * CT + c + 1)
                    wait(pe, xT_ready, (e - 1) * CT + c + 1)
                    turn(6 + c, slot_xn[c], sx_turned)

            def expert(e, k, more):
                def product(dst, a_hi, a_lo, b_hi, b_lo, first, last):
                    for n, (a, b) in enumerate(((a_hi, b_hi), (a_hi, b_lo), (a_lo, b_hi))):
                        ins = pe.matmul(dst, a, b, start=first and n == 0, stop=last and n == 2, skip_group_check=True)
                    return ins

                pe.wait_ge(xT_ready, e * CT + CT)
                for g in range(GP):
                    c = g * WC // GP
                    if g % (GP // WC) == 0:
                        pe.wait_ge(w_ready, e * 2 * WC + c + 1)
                    wait(pe, h_ready, e * GP + g - 3)
                    for f in range(2 * g, 2 * g + 2):
                        cols = slice((f - c * FC) * P, (f - c * FC + 1) * P)
                        for d in range(DK):
                            ins = product(ps[:, g % 4, (f % 2) * C:(f % 2 + 1) * C], w1_hi[c][:, d, cols], w1_lo[c][:, d, cols],
                                          xT_hi[k][:, d, :], xT_lo[k][:, d, :], f % 2 == 0 and d == 0, d == DK - 1)
                    ins.then_inc(h_product, 1)
                if more:
                    turn_slots(e + 1)
                for f in range(FT):
                    w = f // FC
                    if f % FC == 0:
                        pe.wait_ge(w_ready, e * 2 * WC + WC + w + 1)
                    if f % 2 == 0:
                        pe.wait_ge(h_ready, e * GP + f // 2 + 1)
                    for c in range(CT):
                        if f == 0:
                            wait(pe, y_ready, (e - 1) * CT + c + 1)
                        s = slice(c * P, (c + 1) * P)
                        ins = product(ps[:, 4 + c, :], h_hi[:, f, s], h_lo[:, f, s], w2_hi[w][:, f % FC, :], w2_lo[w][:, f % FC, :],
                                      f == 0, f == FT - 1)
                        if f == FT - 1:
                            ins.then_inc(y_product, 1)
                    if f % FC == FC - 1 and f < FT - 1:
                        ins.then_inc(w2_used, 1)
            pe.wait_ge(slots_ready, 1)
            turn_slots(0)
            expert(0, 0, True)
            expert(1, 1, True)
            with pe.Fori(1, E // 2 - 1) as i:
                expert(i * 2, 0, True)
                expert(i * 2 + 1, 1, True)
            expert(E - 2, 0, True)
            expert(E - 1, 1, False)


_INS = ["x", "adj", "L0_gnn_W_seq", "L0_gnn_a1", "L0_gnn_a2", "L0_gnn_W_out", "L0_gnn_b_out",
        "L0_ffn_router_w", "L0_ffn_w1", "L0_ffn_w2"]


def kernel(**inputs):
    import numpy as _np
    import concourse.bacc as _bacc
    from concourse import mybir as _mybir
    from concourse.bass_utils import run_bass_kernel_spmd as _run

    nc = _bacc.Bacc("TRN2", target_bir_lowering=False, num_devices=1)
    arrays, args = {}, []
    for name in _INS:
        a = _np.ascontiguousarray(inputs[name])
        arrays[f"in_{name}_dram"] = a
        args.append(nc.dram_tensor(f"in_{name}_dram", a.shape, _mybir.dt.from_np(a.dtype), kind="ExternalInput").ap())
    out = nc.dram_tensor("out_0_dram", inputs["x"].shape, _mybir.dt.float32, kind="ExternalOutput").ap()
    gnn_moe(nc, *args, out)
    r = _run(nc, [arrays], core_ids=[0])
    return r.results[0]["out_0_dram"]
```

```python
from contextlib import ExitStack

import concourse.bass as bass
from concourse import mybir

ALU = mybir.AluOpType
ACT = mybir.ActivationFunctionType
AX = mybir.AxisListType
F32 = mybir.dt.float32
BF16 = mybir.dt.bfloat16
F16 = mybir.dt.float16
I32 = mybir.dt.int32
U8 = mybir.dt.uint8
F8 = mybir.dt.float8e4
U32 = mybir.dt.uint32
F32R = mybir.dt.float32r

P = 128
EPS = 1e-5
ALPHA = 0.2
LO = 2048.0
SHIFT = 256.0
STEEP = 2.0 ** 100
EDGE = 112.0
OFF = 4096
DVE_TILES = (2, 5, 8, 11, 14)


def live(t, back, tiles):
    return not isinstance(t, int) or 0 <= t - back < tiles


def wait(eng, sem, count):
    if not isinstance(count, int) or count > 0:
        eng.wait_ge(sem, count)


class Steps:

    def __init__(self, eng, sem):
        self.eng, self.sem, self.base, self.n = eng, sem, 0, 0

    def done(self, ins):
        ins.then_inc(self.sem, 1)
        self.n += 1
        self.eng.wait_ge(self.sem, self.base + self.n)


def in_pairs(eng, tiles, first, last, body, steps=None, per=0, by=2):
    for t in range(first):
        body(t, t % by)
    loops = (tiles - first) // by
    if steps:
        start, steps.n, before = steps.base, 0, steps.n
        start = start + before
    with eng.Fori(0, loops) as i:
        for k in range(by):
            if steps:
                steps.base, steps.n = start + i * (by * per) + k * per, 0
            body(i * by + (first + k), k)
            assert not steps or steps.n == per, (steps.n, per)
    if steps:
        steps.base, steps.n = start + loops * by * per, 0
    for t in range(tiles, last):
        body(t, t % by)


def gnn_moe(nc, x, adj, W_seq, a1, a2, W_out, b_out, router_w, w1, w2, out):
    N, D = x.shape
    DH = a1.shape[0]
    H = D // DH
    E, _, F = w1.shape
    C = N // E
    T = N // P
    DK = D // P
    FT = F // P
    CT = C // P
    GP = FT // 2
    WC = 4
    FC = FT // WC
    DC = DH + 1
    VC = 2 * DC
    ROW = D + 4
    ACT_TILES = [j for j in range(T) if j not in DVE_TILES]
    ROW_LOADS = 4
    GROUPS = (slice(0, 12), slice(12, T))
    XB = 4
    NT, NM = 11, 8
    assert len(ACT_TILES) % NT == 0 and T % NM == 0

    s1T_dram = nc.dram_tensor("s1T_dram", (H, N), F32, kind="Internal").ap()
    slots_dram = nc.dram_tensor("slots_dram", (E * C, ROW), F32, kind="Internal").ap()

    with ExitStack() as ctx:
        def sem(name):
            return ctx.enter_context(nc.semaphore(name))

        CONST = 14336
        SIZE = 212608
        arena = ctx.enter_context(nc.sbuf_tensor("arena", [P, SIZE // 4], F32))
        cursor = [0]
        start_of = {}

        def at(offset, name, shape, dt):
            size = {F32: 4, F32R: 4, I32: 4, U32: 4, BF16: 2, F16: 2, U8: 1, F8: 1}[dt]
            n = size
            for s in shape[1:]:
                n *= s
            start_of[name] = offset
            cursor[0] = offset + (n + 31) // 32 * 32
            assert cursor[0] <= SIZE, (name, cursor[0])
            return nc.alloc_sbuf_tensor_at(name, shape, dt, offset=ARENA + offset)

        def after(name, shape, dt):
            return at(cursor[0], name, shape, dt)

        ARENA = 16512

        ident = at(0, "ident", [P, P], F32)
        ident_b = after("ident_b", [P, P], BF16)
        ones = after("ones", [H, P], F32)
        ones_b = after("ones_b", [P, P], BF16)
        earlier_b = after("earlier_b", [P, P], BF16)
        a_bc = after("a_bc", [P, 2, DH], F32)
        scores = after("scores", [P, T, 2 * H], F32)
        uu = after("uu", [P, H, T, 2], F32)
        uuV = after("uuV", [P, H, T, 2], F32)
        AA = after("AA", [P, H, T, 2], F32)
        neg_b = after("neg_b", [P, H, T], F32)
        steep_b = after("steep_b", [P, H, T], F32)
        steep_now = after("steep_now", [P, 2, T], F32)
        bmax = after("bmax", [P, H], F32)
        bmaxT = after("bmaxT", [H, 1], F32)
        bdiag = after("bdiag", [H, H], F32)
        B_bc = after("B_bc", [P, H], F32)
        stats = after("stats", [P, 2, 6], F32)
        mean = after("mean", [P, 2], F32)
        tile_stats = after("tile_stats", [P, T, 6], F32)
        rstd = after("rstd", [P, T], F32)
        newton = [after(f"newton{k}", [P, T], F32) for k in range(2)]
        deg = after("deg", [P, 2], F32)
        lonely = after("lonely", [P, 2], F32)
        router_sb = after("router_sb", [P, DK, E], F32)
        rden = after("rden", [P, 2, H], F32)
        logits = after("logits", [P, T, E], F32)
        rank8 = after("rank8", [P, E], F32)
        first8 = after("first8", [P, E], F32)
        rank8_i = after("rank8_i", [P, E], I32)
        first8_i = after("first8_i", [P, E], I32)
        slot_i = after("slot_i", [P, T], U32)
        assert cursor[0] <= CONST, cursor[0]

        wout_sb = at(CONST, "wout_sb", [P, DK, D], F32)
        bout_bc = after("bout_bc", [P, D], F32)
        MAIN = cursor[0]

        adjT = at(MAIN, "adjT", [P, T, N], U8)
        above = [after(f"above{k}", [P, N], U8) for k in range(len(DVE_TILES))]
        relus = [after(f"relu{k}", [P, N], F8) for k in range(NT)]
        hid = after("hid", [P, T, H, DC], F32)
        tables = [after(f"tables{k}", [P, T, 3 * VC], F16) for k in range(2)]
        value = after("value", [P, T, VC], F32)
        both = after("both", [P, T, VC], F32)
        seq = after("seq", [P, T, D], F32)
        a_row = [after(f"a_row{k}", [P, N], F32) for k in range(2)]
        a_row_end = cursor[0]
        masks = [at(SIZE - (NM - k) * N, f"mask{k}", [P, N], U8) for k in range(NM)]
        assert a_row_end <= start_of["mask0"]

        adj_in = [at(start_of["hid"], "adj_in0", [P, N], F32), after("adj_in1", [P, N], F32)]
        adj_b = [after(f"adj_b{k}", [P, N], BF16) for k in range(2)]
        xn = [after(f"xn{k}", [P, D], F32) for k in range(2)]
        assert cursor[0] <= start_of["tables0"]
        slot_init = at(start_of["tables0"], "slot_init", [P, ROW], F32)
        w_times_a = after("w_times_a", [P, 4, DK, D // 2], F32)
        assert cursor[0] <= start_of["seq"]
        wseq_sb = at(start_of["a_row0"], "wseq_sb", [P, DK, D], F32)
        w_score = after("w_score", [P, DK, 2 * H], F32)
        assert cursor[0] <= start_of["mask0"]
        x_in = [at(start_of["mask0"] + k * D * 4, f"x_in{k}", [P, D], F32) for k in range(XB)]
        HC = D // 2
        wcat_hi = at(start_of["above0"], "wcat_hi", [P, DK, 2, HC + H], F32R)
        wcat_lo = after("wcat_lo", [P, DK, 2, HC + H], F32R)
        xnT_hi = [after(f"xnT_hi{k}", [P, DK, P], F32R) for k in range(2)]
        xnT_lo = [after(f"xnT_lo{k}", [P, DK, P], F32R) for k in range(2)]
        assert cursor[0] <= start_of["hid"]
        s1T = at(start_of["mask0"], "s1T", [H, N], F32)
        assert cursor[0] + 6 * H * T * 4 <= SIZE
        sumB = [after(f"sumB{k}", [P, H, T], F32) for k in range(6)]

        rows = at(MAIN, "rows", [P, T, ROW], F32)
        heads = [after(f"heads{k}", [P, D], F32) for k in range(2)]
        headsT = [after(f"headsT{k}", [P, DK, P], F32) for k in range(2)]
        z = [after(f"z{k}", [P, D], F32) for k in range(2)]
        xn2 = [after(f"xn2_{k}", [P, D], F32) for k in range(2)]
        xn2T = [after(f"xn2T{k}", [P, DK, P], F32) for k in range(2)]
        gap, gap_exp, is_top, one_hot, expert_start = (after(f"rt{k}", [P, T, E], F32) for k in range(5))
        top, first, gap_sum, slot_base, ahead, dropped = (after(f"rt1_{k}", [P, T], F32) for k in range(6))
        oh_b = after("oh_b", [P, T, E], BF16)
        assert cursor[0] <= SIZE - 2 * WC * 2 * FC * D * 4, cursor[0]

        def parts(offset, name, shape):
            raw = at(offset, f"{name}_raw", shape, F32)
            lo = at(offset, f"{name}_lo", shape, F32R)
            return raw, after(f"{name}_hi", shape, F32R), lo

        W_BASE = SIZE - 2 * WC * 2 * FC * D * 4
        w2_raw, w2_hi, w2_lo = zip(*(parts(W_BASE + c * 2 * FC * D * 4, f"w2_{c}", [P, FC, D]) for c in range(WC)))
        w1_raw, w1_hi, w1_lo = zip(*(parts(W_BASE + (WC + c) * 2 * FC * D * 4, f"w1_{c}", [P, DK, F // WC]) for c in range(WC)))
        xT_hi = [at(CONST, "xT_hi0", [P, DK, C], F32R), after("xT_hi1", [P, DK, C], F32R)]
        xT_lo = [after(f"xT_lo{k}", [P, DK, C], F32R) for k in range(2)]
        h_raw, h_hi, h_lo = parts(cursor[0], "h", [P, FT, C])
        slot_rows = [after("slot_rows0", [P, ROW], F32)]
        slot_rows += [after(f"slot_rows{k}", [P, ROW], F32) for k in range(1, 2 * CT)]
        slot_xn = [after(f"slot_xn{k}", [P, D], F32) for k in range(CT)]
        y = [after(f"y{k}", [P, D], F32) for k in range(CT)]
        assert cursor[0] <= W_BASE, (cursor[0], W_BASE)
        ez = [at(start_of["scores"], "ez0", [P, D], F32), at(start_of["uu"], "ez1", [P, D], F32)]
        ps = ctx.enter_context(nc.psum_tensor("ps", [P, 8, 512], F32))
        node_ps = ps[:, :, :].rearrange("p b (i c) -> p (b i) c", i=2)

        pool_step, dve_step = sem("pool_step"), sem("dve_step")
        consts = sem("consts")
        wseq_in, a_in, slot_init_out = sem("wseq_in"), sem("a_in"), sem("slot_init_out")
        x_loaded = [sem(f"x_loaded{k}") for k in range(XB)]
        adj_loaded = [sem(f"adj_loaded{k}") for k in range(2)]
        wa_products = sem("wa_products")
        xn_ready, deg_ready, adjb_ready = sem("xn_ready"), sem("deg_ready"), sem("adjb_ready")
        xn_turned, adj_turned0, adj_turned1 = sem("xn_turned"), sem("adj_turned0"), sem("adj_turned1")
        centered, xnT_hi_ready = sem("centered"), sem("xnT_hi_ready")
        wseq_hi_ready, wseq_ready, w_score_ready = sem("wseq_hi_ready"), sem("wseq_ready"), sem("w_score_ready")
        xnT_ready, adjT_half0, adjT_half1 = sem("xnT_ready"), sem("adjT_half0"), sem("adjT_half1")
        seq_product, seq_ready = sem("seq_product"), sem("seq_ready")
        s1_turned, s1T_ready, s1T_out = sem("s1_turned"), sem("s1T_ready"), sem("s1T_out")
        bmax_ready, bmax_turned = sem("bmax_ready"), sem("bmax_turned")
        bdiag_ready, bmax_spread = sem("bdiag_ready"), sem("bmax_spread")
        var_ready, dev_ready = sem("var_ready"), sem("dev_ready")
        args_ready, exps_ready, factors_ready = sem("args_ready"), sem("exps_ready"), sem("factors_ready")
        a_row_in = [sem(f"a_row_in{k}") for k in range(2)]
        relu_ready, above_ready = sem("relu_ready"), sem("above_ready")
        mask_ready, mask_used = sem("mask_ready"), sem("mask_used")
        value_ready, table_ready = sem("value_ready"), sem("table_ready")
        head_summed, lo_ready, sums_free = sem("head_summed"), sem("lo_ready"), sem("sums_free")
        head_done = sem("head_done")
        post_in, rows_in = sem("post_in"), sem("rows_in")
        heads_ready, heads_turned, headsT_ready = sem("heads_ready"), sem("heads_turned"), sem("headsT_ready")
        proj_product, z_ready, ez_ready = sem("proj_product"), sem("z_ready"), sem("ez_ready")
        mean_ready, row_ready = sem("mean_ready"), sem("row_ready")
        xn2_ready, xn2_turned, xn2T_ready = sem("xn2_ready"), sem("xn2_turned"), sem("xn2T_ready")
        logit_product, logits_ready, x1_out = sem("logit_product"), sem("logits_ready"), sem("x1_out")
        top_gap, top_exp, onehot_ready = sem("top_gap"), sem("top_exp"), sem("onehot_ready")
        counts_ready, slots_ready, scattered = sem("counts_ready"), sem("slots_ready"), sem("scattered")
        token_number = sem("token_number")
        waited = sem("waited")
        w1_in, w2_in = ([sem(f"w{m}_in{c}") for c in range(WC)] for m in (1, 2))
        w_hi_ready, w_ready, w2_used = sem("w_hi_ready"), sem("w_ready"), sem("w2_used")
        xT_hi_ready, h_hi_ready = sem("xT_hi_ready"), sem("h_hi_ready")
        slot_in = [sem(f"slot_in{k}") for k in range(2)]
        sx_ready, sx_turned, xT_ready = sem("sx_ready"), sem("sx_turned"), sem("xT_ready")
        h_product, h_ready, y_product, y_ready = sem("h_product"), sem("h_ready"), sem("y_product"), sem("y_ready")
        y_out = [sem(f"y_out{c}") for c in range(CT)]

        def wait_apart(eng, sem, count):
            wait(eng, sem, count)
            if not isinstance(count, int):
                eng.sem_inc(waited, 1)

        def times_a(eng, i):
            half = slice(i // 2 * (D // 2), (i // 2 + 1) * (D // 2))
            for d in range(DK):
                ins = eng.tensor_tensor(w_times_a[:, i, d, :].rearrange("p (h c) -> p h c", c=DH),
                                        wseq_sb[:, d, half].rearrange("p (h c) -> p h c", c=DH),
                                        a_bc[:, i % 2, :].unsqueeze(1).broadcast_to([P, H // 2, DH]), ALU.mult)
            return ins

        ROUTE_0 = T + 3
        assert GROUPS[0].stop <= ROUTE_0 - 6

        block = ctx.enter_context(nc.Block())

        @block.sync
        def _(sp):
            sp.dma_start(wseq_sb[:], W_seq.rearrange("(k p) n -> p k n", p=P)).then_inc(wseq_in, 16)
            for i, a in enumerate((a1, a2)):
                sp.dma_start(a_bc[:, i, :], a.rearrange("(o d) -> o d", o=1).broadcast_to([P, DH])).then_inc(a_in, 16)
            sp.dma_start(router_sb[:], router_w.rearrange("(k p) e -> p k e", p=P)).then_inc(a_in, 16)

            def load(t, m):
                k = m % 2
                wait(sp, xn_ready, t - XB + 1)
                sp.dma_start(x_in[m][:], x[bass.ds(t * P, P), :]).then_inc(x_loaded[m], 16)
                wait(sp, deg_ready, t - 1)
                sp.dma_start(adj_in[k][:], adj[bass.ds(t * P, P), :]).then_inc(adj_loaded[k], 16)
            in_pairs(sp, T, XB, T, load, by=XB)

            sp.wait_ge(consts, 8)
            sp.dma_start(slots_dram.rearrange("(n p) r -> p n r", p=P),
                         slot_init[:].unsqueeze(1).broadcast_to([P, T, ROW])).then_inc(slot_init_out, 16)
            sp.wait_ge(s1T_ready, 4)
            sp.dma_start(s1T_dram, s1T[:]).then_inc(s1T_out, 16)
            sp.wait_ge(s1T_out, 16)
            sp.wait_ge(slot_init_out, 16)
            sp.wait_ge(seq_ready, T)

            def load_a(h, k):
                wait(sp, mask_ready, (h - 1) * T)
                sp.dma_start(a_row[k][:], s1T_dram[bass.ds(h, 1), :].broadcast_to([P, N])).then_inc(a_row_in[k], 16)
            in_pairs(sp, H, 2, H, load_a)
            sp.dma_start(wout_sb[:], W_out.rearrange("(k p) n -> p k n", p=P)).then_inc(post_in, 16)
            sp.dma_start(bout_bc[:], b_out.rearrange("(o d) -> o d", o=1).broadcast_to([P, D])).then_inc(post_in, 16)

            sp.wait_ge(head_summed, 2 * H)
            sp.wait_ge(head_done, H)
            for q in range(ROW_LOADS):
                n = T // ROW_LOADS
                sp.dma_start(rows[:, q * n:(q + 1) * n, 0:D],
                             x[q * n * P:(q + 1) * n * P, :].rearrange("(t p) d -> p t d", p=P)).then_inc(rows_in, 16)

            def load_w1(e, c):
                sp.dma_start(w1_raw[c][:], w1[bass.ds(e, 1), :, c * (F // WC):(c + 1) * (F // WC)]
                             .rearrange("o (k p) f -> p (o k) f", p=P)).then_inc(w1_in[c], 16)

            def load_w2(e, c):
                sp.dma_start(w2_raw[c][:], w2[bass.ds(e, 1), c * FC * P:(c + 1) * FC * P, :]
                             .rearrange("o (k p) d -> p (o k) d", p=P)).then_inc(w2_in[c], 16)
            for c in range(WC):
                load_w1(0, c)
            load_w2(0, WC - 1)

            def store(t, k):
                sp.wait_ge(row_ready, t + 1)
                sp.dma_start(out[bass.ds(t * P, P), :], rows[:, bass.ds(t, 1), 0:D].rearrange("p o d -> p (o d)")).then_inc(x1_out, 16)
            in_pairs(sp, T, 2, T, store)
            sp.wait_ge(heads_ready, T)
            for c in range(WC - 1):
                load_w2(0, c)

            def load_slots(e, k):
                for c in range(CT):
                    wait(sp, y_out[c], 16 * (e - 1))
                for c in range(CT):
                    sp.dma_start(slot_rows[CT * k + c][:], slots_dram[bass.ds(e * C + c * P, P), :]).then_inc(slot_in[k], 16)
            sp.wait_ge(scattered, 16 * T)
            load_slots(0, 0)
            load_slots(1, 1)

            def refill(e, k, more=True):
                for c in range(WC):
                    sp.wait_ge(h_product, (e - 1) * GP + (c + 1) * (GP // WC))
                    load_w1(e, c)
                for c in range(WC):
                    if c < WC - 1:
                        sp.wait_ge(w2_used, (e - 1) * (WC - 1) + c + 1)
                    else:
                        sp.wait_ge(y_product, e * CT)
                    load_w2(e, c)
                if more:
                    load_slots(e + 1, 1 - k)
            refill(1, 1)
            with sp.Fori(1, E // 2 - 1) as i:
                refill(i * 2, 0)
                refill(i * 2 + 1, 1)
            refill(E - 2, 0)
            refill(E - 1, 1, more=False)
            sp.wait_ge(x1_out, 16 * T)

        @block.gpsimd
        def _(pool):
            pool.memset(ident[:], 0.0).then_inc(pool_step, 1)
            pool.memset(ones_b[:], 1.0).then_inc(consts, 1)
            pool.memset(ones[:], 1.0).then_inc(consts, 1)
            pool.memset(slot_init[:], 0.0).then_inc(pool_step, 1)
            pool.wait_ge(pool_step, 2)
            pool.affine_select(out=ident[:], in_=ident[:], compare_op=ALU.not_equal, fill=1.0, base=0,
                               pattern=[[-1, P]], channel_multiplier=1).then_inc(consts, 1)
            pool.memset(slot_init[:].bitcast(I32)[:, D + 1:D + 2], OFF).then_inc(consts, 1)
            pool.wait_ge(consts, 3)
            pool.tensor_copy(ident_b[:], ident[:]).then_inc(consts, 1)
            pool.affine_select(out=earlier_b[:], in_=ones_b[:], compare_op=ALU.is_gt, fill=0.0, base=0,
                               pattern=[[1, P]], channel_multiplier=-1).then_inc(consts, 1)
            pool.iota(first8_i[:], pattern=[[-1, E]], base=E, channel_multiplier=0).then_inc(consts, 1)
            pool.iota(rank8_i[:], pattern=[[C, E]], base=0, channel_multiplier=0).then_inc(consts, 1)
            pool.wait_ge(wseq_in, 16)
            pool.wait_ge(a_in, 48)
            for i in range(2, 4):
                times_a(pool, i).then_inc(wa_products, 1)
            pool.wait_ge(rows_in, 16 * ROW_LOADS)
            pool.iota(rows[:].bitcast(I32)[:, :, D + 1], pattern=[[P, T]], base=0, channel_multiplier=1).then_inc(token_number, 1)
            pool.wait_ge(token_number, 1)
            for t in range(T):
                for g, s in enumerate(GROUPS):
                    if t == s.start:
                        pool.wait_ge(slots_ready, g + 1)
                        pool.wait_ge(row_ready, s.stop)
                pool.indirect_dma_start(slots_dram, bass.IndirectOffsetOnAxis(slot_i[:, t:t + 1], 0), rows[:, t, :], None,
                                        bounds_check=E * C - 1, oob_is_err=False).then_inc(scattered, 16)
            pool.wait_ge(x1_out, 16 * T)
            for e in range(E):
                for c in range(CT):
                    n = e * CT + c
                    pool.wait_ge(y_ready, n + 1)
                    pool.indirect_dma_start(out, bass.IndirectOffsetOnAxis(slot_rows[n % (2 * CT)][:].bitcast(U32)[:, D + 1:D + 2], 0),
                                            y[c][:], None, bounds_check=N - 1, oob_is_err=False).then_inc(y_out[c], 16)
            for c in range(CT):
                pool.wait_ge(y_out[c], 16 * E)

        @block.scalar
        def _(act):
            act.wait_ge(wseq_in, 16)
            act.activation(wcat_hi[:, :, :, 0:HC], wseq_sb[:].rearrange("p k (g c) -> p k g c", c=HC), ACT.Copy).then_inc(wseq_hi_ready, 1)

            def prepare(t, m):
                k, q = m % 2, 1 - m % 2
                if live(t, 0, T):
                    wait(act, adj_turned1, t - 1)
                    act.wait_ge(adj_loaded[k], (t // 2 + 1) * 16 if isinstance(t, int) else (t - k) * 8 + 16)
                    act.activation(adj_b[k][:], adj_in[k][:], ACT.Copy, accum_out=deg[:, k:k + 1]).then_inc(deg_ready, 1)
                if live(t, 1, T):
                    act.wait_ge(xn_turned, t)
                    wait(act, seq_product, t - 2)
                    act.activation(xnT_hi[q][:].rearrange("p a b -> p (a b)"), ps[:, q, :], ACT.Copy).then_inc(xnT_hi_ready, 1)
                    act.wait_ge(adj_turned0, t)
                    act.activation(adjT[:, 0:T // 2, bass.ds((t - 1) * P, P)],
                                   ps[:, 4, :].bitcast(BF16).rearrange("p (j i) -> p j i", i=P), ACT.Copy).then_inc(adjT_half0, 1)
                if live(t, 3, T):
                    act.wait_ge(seq_product, t - 2)
                    act.activation(seq[:, bass.ds(t - 3, 1), :].rearrange("p o (g c) -> p (o g) c", g=2), ps[:, 2 + 4 * q:4 + 4 * q, 0:HC], ACT.Copy)
                    act.activation(scores[:, bass.ds(t - 3, 1), :].rearrange("p o (g h) -> p (o g) h", g=2),
                                   ps[:, 2 + 4 * q:4 + 4 * q, HC:HC + H], ACT.Copy).then_inc(seq_ready, 1)
            in_pairs(act, T, XB, T + 3, prepare, by=XB)

            act.wait_ge(var_ready, 1)
            act.activation(newton[1][:], newton[0][:], ACT.Sqrt).then_inc(dev_ready, 1)
            for g in range(4):
                act.wait_ge(s1_turned, g + 1)
                act.activation(s1T[:, g * 512:(g + 1) * 512], ps[0:H, g, :], ACT.Copy).then_inc(s1T_ready, 1)
            act.wait_ge(args_ready, 1)
            act.activation(sumB[2][:], sumB[0][:], ACT.Exp).then_inc(exps_ready, 1)
            act.activation(sumB[3][:], sumB[0][:], ACT.Exp, scale=ALPHA).then_inc(exps_ready, 1)
            act.wait_ge(args_ready, 3)
            act.activation(AA[:, :, :, 0], sumB[4][:], ACT.Exp, scale=1.0 - ALPHA).then_inc(exps_ready, 1)
            act.activation(AA[:, :, :, 1], sumB[5][:], ACT.Exp, scale=ALPHA - 1.0).then_inc(exps_ready, 1)

            def evacuate_low(h):
                wait(act, head_done, h)
                for half in range(2):
                    act.wait_ge(head_summed, h * 2 + half + 1)
                    s = slice(half * T // 2, (half + 1) * T // 2)
                    act.activation(both[:, s, :], node_ps[:, s, VC:2 * VC], ACT.Copy, scale=1.0 / LO).then_inc(lo_ready, 1)

            def head(h, k):
                for n, j in enumerate(ACT_TILES):
                    if n == 0:
                        act.wait_ge(a_row_in[k], (h // 2 + 1) * 16 if isinstance(h, int) else (h - k) * 8 + 16)
                        act.wait_ge(value_ready, h + 1)
                    wait_apart(act, mask_ready, (h if n >= NT else h - 1) * T + ACT_TILES[n - NT] + 1)
                    act.activation(relus[n % NT][:], a_row[k][:], ACT.Relu, scale=STEEP, bias=steep_now[:, k, j:j + 1],
                                   saturate=False).then_inc(relu_ready, 1)
                    if n == 3 and live(h, 1, H):
                        evacuate_low(h - 1)
            head(0, 0)
            with act.Fori(0, (H - 2) // 2) as i:
                head(i * 2 + 1, 1)
                head(i * 2 + 2, 0)
            head(H - 1, 1)
            evacuate_low(H - 1)

            def post(t, k):
                q = 1 - k
                if live(t, 0, T):
                    act.wait_ge(heads_turned, t + 1)
                    wait(act, proj_product, t - 1)
                    act.activation(headsT[k][:].rearrange("p a b -> p (a b)"), ps[:, k, :], ACT.Copy).then_inc(headsT_ready, 1)
                if live(t, 5, T):
                    act.wait_ge(xn2_turned, t - 4)
                    wait(act, logit_product, t - 6)
                    act.activation(xn2T[q][:].rearrange("p a b -> p (a b)"), ps[:, 4 + q, :], ACT.Copy).then_inc(xn2T_ready, 1)
                if live(t, 3, T):
                    act.wait_ge(z_ready, t - 2)
                    wait(act, row_ready, t - 4)
                    act.activation(ez[q][:], z[q][:], ACT.Exp).then_inc(ez_ready, 1)
                if live(t, 4, T):
                    act.wait_ge(mean_ready, t - 3)
                    wait(act, xn2_turned, t - 5)
                    act.activation(xn2[k][:], ez[k][:], ACT.Identity, bias=mean[:, k:k + 1]).then_inc(xn2_ready, 1)
                    act.activation(rows[:, bass.ds(t - 4, 1), 0:D].rearrange("p o d -> p (o d)"), ez[k][:], ACT.Copy).then_inc(row_ready, 1)
                if isinstance(t, int) and t == ROUTE_0:
                    act.wait_ge(var_ready, 2)
                    act.activation(newton[1][:], newton[0][:], ACT.Sqrt).then_inc(dev_ready, 1)
                    gap_exps(0)

            def gap_exps(g):
                act.wait_ge(top_gap, g + 1)
                act.activation(gap_exp[:, GROUPS[g], :], gap[:, GROUPS[g], :], ACT.Exp).then_inc(top_exp, 1)
            in_pairs(act, T, 8, T + 7, post)
            gap_exps(1)

            def turn_slots(e, k):
                for c in range(CT):
                    act.wait_ge(sx_turned, e * CT + c + 1)
                    act.activation(xT_hi[k][:, :, c * P:(c + 1) * P],
                                   ps[:, 6 + c, :].rearrange("p (a b) -> p a b", b=P), ACT.Copy).then_inc(xT_hi_ready, 1)

            def first_part(hi, raw, loaded, e):
                act.wait_ge(loaded, e * 16 + 16)
                act.activation(hi[:], raw[:], ACT.Copy).then_inc(w_hi_ready, 1)

            def expert(e, k, more):
                for g in range(GP):
                    act.wait_ge(h_product, e * GP + g + 1)
                    for dst in (h_raw, h_hi):
                        ins = act.activation(dst[:, 2 * g:2 * g + 2, :].rearrange("p a b -> p (a b)"), ps[:, g % 4, :], ACT.Gelu_apprx_tanh)
                    ins.then_inc(h_hi_ready, 1)
                    if g % 2 == 0:
                        first_part(w2_hi[g // 2], w2_raw[g // 2], w2_in[g // 2], e)
                if more:
                    turn_slots(e + 1, 1 - k)
                    for c in range(WC):
                        first_part(w1_hi[c], w1_raw[c], w1_in[c], e + 1)
            for c in range(WC):
                first_part(w1_hi[c], w1_raw[c], w1_in[c], 0)
            turn_slots(0, 0)
            expert(0, 0, True)
            expert(1, 1, True)
            with act.Fori(1, E // 2 - 1) as i:
                expert(i * 2, 0, True)
                expert(i * 2 + 1, 1, True)
            expert(E - 2, 0, True)
            expert(E - 1, 1, False)

        @block.vector
        def _(dve):
            steps = Steps(dve, dve_step)

            def copy(dst, src):
                return dve.tensor_scalar(dst, src, 1.0, None, ALU.mult)

            def negative_mean(src, k, t, used, count, ready):
                st = stats[:, k, :]
                steps.done(dve.bn_stats(st, src))
                copy(tile_stats[:, bass.ds(t, 1), :].rearrange("p o c -> p (o c)"), st)
                wait(dve, used, count)
                dve.tensor_scalar(mean[:, k:k + 1], st[:, 1:2], st[:, 4:5], -0.5, ALU.add, ALU.mult).then_inc(ready, 1)

            def variance():
                st, a, b = tile_stats, newton[0][:], newton[1][:]
                steps.done(dve.tensor_tensor(a, st[:, :, 2], st[:, :, 5], ALU.add))
                steps.done(dve.tensor_scalar(a, a, 1.0 / D, EPS, ALU.mult, ALU.add))
                steps.done(dve.tensor_tensor(b, st[:, :, 1], st[:, :, 4], ALU.subtract))
                steps.done(dve.tensor_tensor(b, b, b, ALU.mult))
                dve.scalar_tensor_tensor(out=a, in0=b, scalar=0.25, in1=a, op0=ALU.mult, op1=ALU.add).then_inc(var_ready, 1)

            def inverse_deviation(nth):
                a, b, r = newton[0][:], newton[1][:], rstd[:]
                dve.wait_ge(dev_ready, nth)
                steps.done(dve.reciprocal(r, b))
                steps.done(dve.tensor_tensor(b, r, r, ALU.mult))
                steps.done(dve.scalar_tensor_tensor(out=b, in0=b, scalar=-0.5, in1=a, op0=ALU.mult, op1=ALU.mult))
                steps.done(dve.scalar_tensor_tensor(out=r, in0=b, scalar=1.5, in1=r, op0=ALU.add, op1=ALU.mult))

            def sum_w_times_a(i):
                for d in range(DK):
                    ins = dve.tensor_reduce(w_score[:, d, (i % 2) * H + (i // 2) * (H // 2):(i % 2) * H + (i // 2 + 1) * (H // 2)],
                                            w_times_a[:, i, d, :].rearrange("p (h c) -> p h c", c=DH), AX.X, ALU.add)
                return ins
            dve.wait_ge(wseq_in, 16)
            dve.wait_ge(a_in, 48)
            for i in range(2):
                steps.done(times_a(dve, i))
                sum_w_times_a(i)

            def prepare(t, m):
                k, q = m % 2, 1 - m % 2
                if live(t, 0, T):
                    dve.wait_ge(x_loaded[m], (t // XB + 1) * 16 if isinstance(t, int) else (t - m) * (16 // XB) + 16)
                    negative_mean(x_in[m][:], k, t, xn_ready, t - 1, centered)
                    dve.wait_ge(centered, t + 1)
                    wait(dve, xn_turned, t - 1)
                    dve.tensor_scalar(xn[k][:], x_in[m][:], mean[:, k:k + 1], None, ALU.add).then_inc(xn_ready, 1)
                    if isinstance(t, int) and t == 0:
                        dve.wait_ge(wseq_hi_ready, 1)
                        dve.tensor_tensor(wcat_lo[:, :, :, 0:HC], wseq_sb[:].rearrange("p k (g c) -> p k g c", c=HC),
                                          wcat_hi[:, :, :, 0:HC].bitcast(F32), ALU.subtract).then_inc(wseq_ready, 1)
                    dve.wait_ge(deg_ready, t + 1)
                    steps.done(dve.tensor_scalar(lonely[:, k:k + 1], deg[:, k:k + 1], 0.0, None, ALU.is_equal))
                    dve.tensor_scalar(adj_b[k][:], adj_b[k][:], lonely[:, k:k + 1], EDGE, ALU.add, ALU.mult).then_inc(adjb_ready, 1)
                if live(t, 1, T):
                    dve.wait_ge(xnT_hi_ready, t)
                    wait(dve, seq_product, t - 2)
                    dve.tensor_tensor(xnT_lo[q][:].rearrange("p a b -> p (a b)"), ps[:, q, :],
                                      xnT_hi[q][:].rearrange("p a b -> p (a b)").bitcast(F32), ALU.subtract).then_inc(xnT_ready, 1)
                    dve.wait_ge(adj_turned1, t)
                    copy(adjT[:, T // 2:T, bass.ds((t - 1) * P, P)],
                         ps[:, 5, :].bitcast(BF16).rearrange("p (j i) -> p j i", i=P)).then_inc(adjT_half1, 1)
                if isinstance(t, int) and t == 1:
                    for i in range(2, 4):
                        dve.wait_ge(wa_products, i - 1)
                        ins = sum_w_times_a(i)
                    steps.done(ins)
                    ws = w_score[:].rearrange("p k (g h) -> p k g h", g=2)
                    steps.done(copy(wcat_hi[:, :, :, HC:HC + H], ws))
                    dve.tensor_tensor(wcat_lo[:, :, :, HC:HC + H], ws, wcat_hi[:, :, :, HC:HC + H].bitcast(F32), ALU.subtract).then_inc(w_score_ready, 1)
            in_pairs(dve, T, XB, T + 3, prepare, steps, 2, by=XB)

            variance()
            inverse_deviation(1)
            dve.wait_ge(seq_ready, T)
            steps.done(dve.tensor_tensor(scores[:], scores[:], rstd[:].unsqueeze(2).broadcast_to([P, T, 2 * H]), ALU.mult))
            dve.tensor_reduce(bmax[:], scores[:, :, H:2 * H].rearrange("p t h -> p h t"), AX.X, ALU.max).then_inc(bmax_ready, 1)
            dve.wait_ge(bmax_turned, 1)
            steps.done(dve.tensor_reduce(bmaxT[:], ps[0:H, 4, 0:P], AX.X, ALU.max))
            dve.tensor_scalar(bdiag[:], ident[0:H, 0:H], bmaxT[:, 0:1], None, ALU.mult).then_inc(bdiag_ready, 1)
            dve.wait_ge(bmax_spread, 1)
            steps.done(dve.tensor_copy(B_bc[:], ps[:, 5, 0:H]))
            B_all = B_bc[:].unsqueeze(2).broadcast_to([P, H, T])
            s1 = scores[:, :, 0:H].rearrange("p t h -> p h t")
            s2 = scores[:, :, H:2 * H].rearrange("p t h -> p h t")
            dve.tensor_tensor(sumB[0][:], s2, B_all, ALU.subtract).then_inc(args_ready, 1)
            steps.done(dve.tensor_tensor(sumB[1][:], s1, B_all, ALU.add))
            dve.tensor_scalar(sumB[4][:], sumB[1][:], 0.0, None, ALU.min).then_inc(args_ready, 1)
            dve.tensor_scalar(sumB[5][:], sumB[1][:], 0.0, None, ALU.max).then_inc(args_ready, 1)
            dve.tensor_scalar(neg_b[:], s2, -1.0, None, ALU.mult)
            dve.tensor_scalar(steep_b[:], s2, STEEP, None, ALU.mult).then_inc(factors_ready, 1)
            dve.wait_ge(exps_ready, 2)
            dve.tensor_scalar(uu[:, :, :, 0], sumB[2][:], SHIFT * LO, None, ALU.mult)
            steps.done(dve.tensor_scalar(uu[:, :, :, 1], sumB[3][:], -SHIFT * LO, None, ALU.mult))
            steps.done(dve.tensor_tensor(uuV[:], uu[:], rstd[:].unsqueeze(1).unsqueeze(3).broadcast_to([P, H, T, 2]), ALU.mult))

            def values(h, k):
                dve.tensor_scalar(steep_now[:, k, :], steep_b[:, bass.ds(h, 1), :].rearrange("p o t -> p (o t)"), 1.0, None, ALU.mult)
                v = value[:].rearrange("p t (b c) -> p t b c", b=2)
                u, uV = (a[:, bass.ds(h, 1), :, :].rearrange("p o t b -> p (o t) b") for a in (uu, uuV))
                dve.tensor_tensor(v[:, :, :, 0:DH], seq[:, :, bass.ds(h * DH, DH)].unsqueeze(2).broadcast_to([P, T, 2, DH]),
                                  uV.unsqueeze(3).broadcast_to([P, T, 2, DH]), ALU.mult)
                dve.tensor_copy(v[:, :, :, DH], u).then_inc(value_ready, 1)

            def split(h, k):
                dve.wait_ge(value_ready, h + 1)
                tb = tables[k]
                steps.done(dve.tensor_scalar(tb[:, :, 0:VC], value[:], 1.0 / LO, None, ALU.mult))
                steps.done(dve.scalar_tensor_tensor(out=tb[:, :, VC:2 * VC], in0=tb[:, :, 0:VC], scalar=-LO, in1=value[:],
                                                    op0=ALU.mult, op1=ALU.add))
                dve.tensor_scalar(tb[:, :, 2 * VC:3 * VC].rearrange("p t (b c) -> p t b c", b=2),
                                  tb[:, :, 0:2 * VC].rearrange("p t (b c) -> p t b c", b=2)[:, :, :, DC:VC],
                                  -1.0, None, ALU.mult).then_inc(table_ready, 1)

            def combine(h):
                for half in range(2):
                    s = slice(half * T // 2, (half + 1) * T // 2)
                    dve.wait_ge(lo_ready, h * 2 + half + 1)
                    ins = dve.tensor_tensor(both[:, s, :], node_ps[:, s, 0:VC], both[:, s, :], ALU.add).then_inc(sums_free, 1)

            def weigh(h):
                dve.wait_ge(sums_free, h * 2 + 4)
                b4 = both[:].rearrange("p t (b c) -> p t b c", b=2)
                A = AA[:, bass.ds(h, 1), :, :].rearrange("p o t b -> p (o t) b").unsqueeze(3).broadcast_to([P, T, 2, DC])
                steps.done(dve.tensor_tensor(b4, b4, A, ALU.mult))
                dve.tensor_tensor(hid[:, :, bass.ds(h, 1), :].rearrange("p t o c -> p t (o c)"), b4[:, :, 0, :], b4[:, :, 1, :],
                                  ALU.add).then_inc(head_done, 1)

            dve.sem_inc(sums_free, 2)
            dve.wait_ge(slot_init_out, 16)
            values(0, 0)
            split(0, 0)
            dve.wait_ge(factors_ready, 1)
            dve.wait_ge(adjT_half0, T)
            dve.wait_ge(adjT_half1, T)
            dve.wait_ge(exps_ready, 4)
            dve.wait_ge(s1T_out, 16)

            def head(h, k):
                def compare(d):
                    j = DVE_TILES[d]
                    dve.tensor_scalar(above[d][:], a_row[k][:], neg_b[:, bass.ds(h, 1), j:j + 1].rearrange("p o q -> p (o q)"),
                                      EDGE, ALU.is_gt, ALU.mult).then_inc(above_ready, 1)

                dve.wait_ge(a_row_in[k], (h // 2 + 1) * 16 if isinstance(h, int) else (h - k) * 8 + 16)
                r = d = 0
                for j in range(T):
                    if j < NM:
                        wait(dve, mask_used, h * T + j + 1 - NM)
                    else:
                        dve.wait_ge(mask_used, h * T + j + 1 - NM)
                    if j in DVE_TILES:
                        dve.wait_ge(above_ready, h * len(DVE_TILES) + d + 1)
                        source, d = above[d], d + 1
                    else:
                        dve.wait_ge(relu_ready, h * len(ACT_TILES) + r + 1)
                        source, r = relus[r % NT], r + 1
                    dve.tensor_tensor(masks[j % NM][:].bitcast(I32), source[:].bitcast(I32), adjT[:, j, :].bitcast(I32),
                                      ALU.bitwise_and).then_inc(mask_ready, 1)
                    if j == 3 and live(h, 1, H):
                        combine(h - 1)
                    if j == 7 and live(h, 1, H):
                        weigh(h - 1)
                    if j == 0 or j - 1 in DVE_TILES and d < len(DVE_TILES):
                        compare(d)
                    if not isinstance(h, int) or h + 1 < H:
                        if j == 9:
                            values(h + 1, 1 - k)
                        if j == 12:
                            split(h + 1, 1 - k)
            head(0, 0)
            per = 3
            start = steps.base + steps.n
            with dve.Fori(0, (H - 2) // 2) as i:
                for k in range(2):
                    steps.base, steps.n = start + i * (2 * per) + k * per, 0
                    head(i * 2 + (1 + k), 1 - k)
                    assert steps.n == per
            steps.base, steps.n = start + (H - 2) * per, 0
            head(H - 1, 1)
            combine(H - 1)
            weigh(H - 1)

            dve.wait_ge(head_done, H)
            dve.wait_ge(post_in, 32)

            def post(t, k):
                q = 1 - k
                if live(t, 7, T):
                    dve.wait_ge(logit_product, t - 6)
                    copy(logits[:, bass.ds(t - 7, 1), :].rearrange("p o e -> p (o e)"), ps[:, 6 + q, 0:E]).then_inc(logits_ready, 1)
                if live(t, 0, T):
                    hd = hid[:, bass.ds(t, 1), :, :].rearrange("p o h c -> p (o h) c")
                    steps.done(dve.reciprocal(rden[:, k, :], hd[:, :, DH]))
                    wait(dve, heads_turned, t - 1)
                    dve.tensor_tensor(heads[k][:].rearrange("p (h c) -> p h c", c=DH), hd[:, :, 0:DH],
                                      rden[:, k, :].unsqueeze(2).broadcast_to([P, H, DH]), ALU.mult).then_inc(heads_ready, 1)
                if live(t, 3, T):
                    dve.wait_ge(proj_product, t - 2)
                    dve.tensor_tensor(z[q][:], ps[:, 2 + q, :], bout_bc[:], ALU.add).then_inc(z_ready, 1)
                if live(t, 4, T):
                    if isinstance(t, int) and t == 4:
                        dve.wait_ge(rows_in, 16 * ROW_LOADS)
                    row = rows[:, bass.ds(t - 4, 1), 0:D].rearrange("p o d -> p (o d)")
                    dve.wait_ge(ez_ready, t - 3)
                    steps.done(dve.tensor_scalar(ez[k][:], ez[k][:], 1.0, -1.0, ALU.min, ALU.add))
                    steps.done(dve.scalar_tensor_tensor(out=ez[k][:], in0=z[k][:], scalar=0.0, in1=ez[k][:], op0=ALU.max, op1=ALU.add))
                    steps.done(dve.tensor_tensor(ez[k][:], row, ez[k][:], ALU.add))
                    negative_mean(ez[k][:], k, t - 4, xn2_ready, t - 5, mean_ready)
                if isinstance(t, int) and t == ROUTE_0:
                    dve.wait_ge(mean_ready, T)
                    variance()
                    choose(0)
                    seat(0)
                    inverse_deviation(2)
                    steps.done(dve.tensor_tensor(newton[0][:], tile_stats[:, :, 1], tile_stats[:, :, 4], ALU.add))
                    dve.tensor_scalar(rows[:, :, D + 2], newton[0][:], 0.5, None, ALU.mult)
                    steps.done(dve.tensor_copy(rows[:, :, D + 3], rstd[:]))
                    gate(0)

            def each(a, s):
                return a[:, s].unsqueeze(2).broadcast_to([P, s.stop - s.start, E])

            def experts(a, s):
                return a[:].unsqueeze(1).broadcast_to([P, s.stop - s.start, E])

            def choose(g):
                s = GROUPS[g]
                dve.wait_ge(logits_ready, s.stop)
                steps.done(dve.tensor_reduce(top[:, s], logits[:, s, :], AX.X, ALU.max))
                steps.done(dve.tensor_tensor(is_top[:, s, :], logits[:, s, :], each(top, s), ALU.is_equal))
                dve.tensor_tensor(gap[:, s, :], logits[:, s, :], each(top, s), ALU.subtract)
                steps.done(dve.tensor_tensor(is_top[:, s, :], is_top[:, s, :], experts(first8, s), ALU.mult))
                steps.done(dve.tensor_reduce(first[:, s], is_top[:, s, :], AX.X, ALU.max))
                steps.done(dve.tensor_tensor(one_hot[:, s, :], is_top[:, s, :], each(first, s), ALU.is_equal))
                dve.tensor_copy(oh_b[:, s, :], one_hot[:, s, :]).then_inc(onehot_ready, 1)
                steps.done(dve.tensor_tensor(expert_start[:, s, :], one_hot[:, s, :], experts(rank8, s), ALU.mult))
                dve.tensor_reduce(slot_base[:, s], expert_start[:, s, :], AX.X, ALU.add)

            def seat(g):
                s = GROUPS[g]
                dve.wait_ge(counts_ready, g + 1)
                steps.done(dve.tensor_tensor(is_top[:, s, :], ps[:, 0, s.start * E:s.stop * E].rearrange("p (t e) -> p t e", e=E),
                                             one_hot[:, s, :], ALU.mult))
                steps.done(dve.tensor_reduce(ahead[:, s], is_top[:, s, :], AX.X, ALU.add))
                dve.tensor_tensor(slot_base[:, s], slot_base[:, s], ahead[:, s], ALU.add)
                steps.done(dve.tensor_scalar(dropped[:, s], ahead[:, s], float(C), float(OFF), ALU.is_ge, ALU.mult))
                dve.tensor_tensor(slot_i[:, s], slot_base[:, s], dropped[:, s], ALU.add)

            def gate(g):
                s = GROUPS[g]
                dve.tensor_tensor(gap[:, s, :], gap[:, s, :], each(rstd, s), ALU.mult).then_inc(top_gap, 1)
                dve.wait_ge(top_exp, g + 1)
                steps.done(dve.tensor_reduce(gap_sum[:, s], gap_exp[:, s, :], AX.X, ALU.add))
                dve.reciprocal(rows[:, s, D], gap_sum[:, s]).then_inc(slots_ready, 1)

            dve.tensor_copy(first8[:], first8_i[:])
            dve.tensor_copy(rank8[:], rank8_i[:])
            in_pairs(dve, T, 8, T + 7, post, steps, 5)
            choose(1)
            seat(1)
            gate(1)

            def norm_slots(e, k):
                dve.wait_ge(slot_in[k], (e // 2 + 1) * 16 * CT if isinstance(e, int) else (e - k) * 8 * CT + 16 * CT)
                for c in range(CT):
                    wait(dve, sx_turned, (e - 1) * CT + c + 1)
                    r = slot_rows[CT * k + c]
                    dve.tensor_scalar(slot_xn[c][:], r[:, 0:D], r[:, D + 2:D + 3], r[:, D + 3:D + 4], ALU.subtract, ALU.mult).then_inc(sx_ready, 1)

            def second_part(lo, raw, hi, count):
                dve.wait_ge(w_hi_ready, count)
                dve.tensor_tensor(lo[:], raw[:], hi[:].bitcast(F32), ALU.subtract).then_inc(w_ready, 1)

            def turn_slots(e, k):
                for c in range(CT):
                    s = slice(c * P, (c + 1) * P)
                    dve.wait_ge(xT_hi_ready, e * CT + c + 1)
                    dve.tensor_tensor(xT_lo[k][:, :, s], ps[:, 6 + c, :].rearrange("p (a b) -> p a b", b=P),
                                      xT_hi[k][:, :, s].bitcast(F32), ALU.subtract).then_inc(xT_ready, 1)

            def expert(e, k, more):
                for g in range(GP):
                    pair = slice(2 * g, 2 * g + 2)
                    dve.wait_ge(h_hi_ready, e * GP + g + 1)
                    dve.tensor_tensor(h_lo[:, pair, :], h_raw[:, pair, :], h_hi[:, pair, :].bitcast(F32), ALU.subtract).then_inc(h_ready, 1)
                    if g % 2 == 0:
                        second_part(w2_lo[g // 2], w2_raw[g // 2], w2_hi[g // 2], e * 2 * WC + WC + g // 2 + 1)
                    if g == 3 and more:
                        norm_slots(e + 1, 1 - k)
                if more:
                    turn_slots(e + 1, 1 - k)
                    for c in range(WC):
                        second_part(w1_lo[c], w1_raw[c], w1_hi[c], (e + 1) * 2 * WC + c + 1)
                for c in range(CT):
                    dve.wait_ge(y_product, e * CT + c + 1)
                    wait(dve, y_out[c], e * 16)
                    r = slot_rows[CT * k + c]
                    dve.scalar_tensor_tensor(out=y[c][:], in0=ps[:, 4 + c, :], scalar=r[:, D:D + 1], in1=r[:, 0:D],
                                             op0=ALU.mult, op1=ALU.add).then_inc(y_ready, 1)
            for c in range(WC):
                second_part(w1_lo[c], w1_raw[c], w1_hi[c], c + 1)
            norm_slots(0, 0)
            turn_slots(0, 0)
            expert(0, 0, True)
            expert(1, 1, True)
            with dve.Fori(1, E // 2 - 1) as i:
                expert(i * 2, 0, True)
                expert(i * 2 + 1, 1, True)
            expert(E - 2, 0, True)
            expert(E - 1, 1, False)

        @block.tensor
        def _(pe):
            pe.wait_ge(consts, 8)

            def turn(dst_bank, src, ready):
                for d in range(DK):
                    ins = pe.transpose(ps[:, dst_bank, d * P:(d + 1) * P], src[:, d * P:(d + 1) * P], ident[:])
                ins.then_inc(ready, 1)

            def product(dst, a_hi, a_lo, b_hi, b_lo, first, last):
                for n, (a, b) in enumerate(((a_hi, b_hi), (a_hi, b_lo), (a_lo, b_hi))):
                    ins = pe.matmul(dst, a, b, start=first and n == 0, stop=last and n == 2, skip_group_check=True)
                return ins

            def prepare(t, k):
                q = 1 - k
                if live(t, 1, T):
                    pe.wait_ge(xn_ready, t)
                    wait(pe, xnT_ready, t - 2)
                    turn(q, xn[q], xn_turned)
                    pe.wait_ge(adjb_ready, t)
                    for half, (left, turned) in enumerate(((adjT_half0, adj_turned0), (adjT_half1, adj_turned1))):
                        wait(pe, left, t - 1)
                        bank = ps[:, 4 + half, :].bitcast(BF16)
                        for j in range(T // 2):
                            jt = half * (T // 2) + j
                            ins = pe.transpose(bank[:, j * P:(j + 1) * P], adj_b[q][:, jt * P:(jt + 1) * P], ident_b[:])
                        ins.then_inc(turned, 1)
                if live(t, 2, T):
                    if isinstance(t, int) and t == 2:
                        pe.wait_ge(wseq_ready, 1)
                    pe.wait_ge(xnT_ready, t - 1)
                    wait(pe, seq_ready, t - 3)
                    if isinstance(t, int) and t == 2:
                        pe.wait_ge(w_score_ready, 1)
                    for g in range(2):
                        for d in range(DK):
                            ins = product(ps[:, 2 + 4 * k + g, 0:HC + H], xnT_hi[k][:, d, :], xnT_lo[k][:, d, :],
                                          wcat_hi[:, d, g, :], wcat_lo[:, d, g, :], d == 0, d == DK - 1)
                    ins.then_inc(seq_product, 1)
            in_pairs(pe, T, 4, T + 3, prepare)

            pe.wait_ge(seq_ready, T)
            pe.wait_ge(adjT_half0, T)
            pe.wait_ge(adjT_half1, T)
            pe.wait_ge(bmax_ready, 1)
            pe.transpose(ps[0:H, 4, 0:P], bmax[:], ident[:]).then_inc(bmax_turned, 1)
            for g in range(4):
                for t in range(4 * g, 4 * g + 4):
                    ins = pe.transpose(ps[0:H, g, (t % 4) * P:(t % 4 + 1) * P], scores[:, t, 0:H], ident[:])
                ins.then_inc(s1_turned, 1)
                if g == 0:
                    pe.wait_ge(bdiag_ready, 1)
                    pe.matmul(ps[:, 5, 0:H], ones[:], bdiag[:], start=True, stop=True).then_inc(bmax_spread, 1)
            pe.wait_ge(s1T_ready, 4)
            pe.wait_ge(value_ready, 1)

            with pe.Fori(0, H // 2) as i:
                for k in range(2):
                    h = i * 2 + k
                    wait_apart(pe, table_ready, h + 1)
                    tb = tables[k]
                    for half, j in ((b, a + c) for a in range(0, T, 2) for b in range(2) for c in range(2)):
                        if half == 0:
                            wait_apart(pe, mask_ready, h * T + j + 1)
                        if j == 0:
                            wait_apart(pe, sums_free, h * 2 + 1 + half)
                        for n in range(half * T // 2, (half + 1) * T // 2):
                            cols = slice(n * P, (n + 1) * P)
                            ins = pe.matmul(node_ps[:, n, 0:2 * VC], masks[j % NM][:, cols].bitcast(F8), tb[:, j, 0:2 * VC],
                                            start=(j == 0 and n % 2 == 0), stop=False, skip_group_check=True)
                            if n == T - 1:
                                ins.then_inc(mask_used, 1)
                            ins = pe.matmul(node_ps[:, n, 0:2 * VC].rearrange("p (b c) -> p b c", b=2)[:, :, DC:VC],
                                            adjT[:, j, cols].bitcast(F8), tb[:, j, 2 * VC:3 * VC].rearrange("p (b c) -> p b c", b=2),
                                            start=False, stop=(j == T - 1), skip_group_check=True)
                        if j == T - 1:
                            ins.then_inc(head_summed, 1)

            pe.wait_ge(post_in, 32)
            pe.wait_ge(sums_free, 2 * H + 2)

            def post(t, k):
                q = 1 - k
                if live(t, 2, T):
                    pe.wait_ge(headsT_ready, t - 1)
                    wait(pe, z_ready, t - 3)
                    for d in range(DK):
                        ins = pe.matmul(ps[:, 2 + k, :], headsT[k][:, d, :], wout_sb[:, d, :], start=(d == 0), stop=(d == DK - 1))
                    ins.then_inc(proj_product, 1)
                if live(t, 6, T):
                    pe.wait_ge(xn2T_ready, t - 5)
                    wait(pe, logits_ready, t - 7)
                    for d in range(DK):
                        ins = pe.matmul(ps[:, 6 + k, 0:E], xn2T[k][:, d, :], router_sb[:, d, :], start=(d == 0), stop=(d == DK - 1))
                    ins.then_inc(logit_product, 1)
                if live(t, 0, T):
                    pe.wait_ge(heads_ready, t + 1)
                    wait(pe, headsT_ready, t - 1)
                    turn(k, heads[k], heads_turned)
                if live(t, 5, T):
                    pe.wait_ge(xn2_ready, t - 4)
                    wait(pe, xn2T_ready, t - 6)
                    turn(4 + q, xn2[q], xn2_turned)
                if isinstance(t, int) and t == ROUTE_0:
                    count(0)

            def count(g):
                s = GROUPS[g]
                n = s.stop - s.start
                counts = ps[:, 0, s.start * E:s.stop * E].rearrange("p (t e) -> p t e", e=E)
                pe.wait_ge(onehot_ready, g + 1)
                pe.matmul(counts, earlier_b[:], oh_b[:, s, :], start=True, stop=False, skip_group_check=True)
                for t in range(s.stop - 1):
                    behind = max(t + 1 - s.start, 0)
                    ins = pe.matmul(counts[:, behind:n, :], ones_b[:], oh_b[:, t:t + 1, :].broadcast_to([P, n - behind, E]),
                                    start=False, stop=(t == s.stop - 2), skip_group_check=True)
                ins.then_inc(counts_ready, 1)
            in_pairs(pe, T, 8, T + 7, post)
            count(1)

            def turn_slots(e):
                for c in range(CT):
                    pe.wait_ge(sx_ready, e * CT + c + 1)
                    wait(pe, xT_ready, (e - 1) * CT + c + 1)
                    turn(6 + c, slot_xn[c], sx_turned)

            def expert(e, k, more):
                pe.wait_ge(xT_ready, e * CT + CT)
                for g in range(GP):
                    c = g * WC // GP
                    if g % (GP // WC) == 0:
                        pe.wait_ge(w_ready, e * 2 * WC + c + 1)
                    wait(pe, h_ready, e * GP + g - 3)
                    for f in range(2 * g, 2 * g + 2):
                        cols = slice((f - c * FC) * P, (f - c * FC + 1) * P)
                        for d in range(DK):
                            ins = product(ps[:, g % 4, (f % 2) * C:(f % 2 + 1) * C], w1_hi[c][:, d, cols], w1_lo[c][:, d, cols],
                                          xT_hi[k][:, d, :], xT_lo[k][:, d, :], f % 2 == 0 and d == 0, d == DK - 1)
                    ins.then_inc(h_product, 1)
                if more:
                    turn_slots(e + 1)
                for f in range(FT):
                    w = f // FC
                    if f % FC == 0:
                        pe.wait_ge(w_ready, e * 2 * WC + WC + w + 1)
                    if f % 2 == 0:
                        pe.wait_ge(h_ready, e * GP + f // 2 + 1)
                    for c in range(CT):
                        if f == 0:
                            wait(pe, y_ready, (e - 1) * CT + c + 1)
                        s = slice(c * P, (c + 1) * P)
                        ins = product(ps[:, 4 + c, :], h_hi[:, f, s], h_lo[:, f, s], w2_hi[w][:, f % FC, :], w2_lo[w][:, f % FC, :],
                                      f == 0, f == FT - 1)
                        if f == FT - 1:
                            ins.then_inc(y_product, 1)
                    if f % FC == FC - 1 and f < FT - 1:
                        ins.then_inc(w2_used, 1)
            pe.wait_ge(slots_ready, len(GROUPS))
            turn_slots(0)
            expert(0, 0, True)
            expert(1, 1, True)
            with pe.Fori(1, E // 2 - 1) as i:
                expert(i * 2, 0, True)
                expert(i * 2 + 1, 1, True)
            expert(E - 2, 0, True)
            expert(E - 1, 1, False)


_INS = ["x", "adj", "L0_gnn_W_seq", "L0_gnn_a1", "L0_gnn_a2", "L0_gnn_W_out", "L0_gnn_b_out",
        "L0_ffn_router_w", "L0_ffn_w1", "L0_ffn_w2"]


def kernel(**inputs):
    import numpy as _np
    import concourse.bacc as _bacc
    from concourse import mybir as _mybir
    from concourse.bass_utils import run_bass_kernel_spmd as _run

    nc = _bacc.Bacc("TRN2", target_bir_lowering=False, num_devices=1)
    arrays, args = {}, []
    for name in _INS:
        a = _np.ascontiguousarray(inputs[name])
        arrays[f"in_{name}_dram"] = a
        args.append(nc.dram_tensor(f"in_{name}_dram", a.shape, _mybir.dt.from_np(a.dtype), kind="ExternalInput").ap())
    out = nc.dram_tensor("out_0_dram", inputs["x"].shape, _mybir.dt.float32, kind="ExternalOutput").ap()
    gnn_moe(nc, *args, out)
    r = _run(nc, [arrays], core_ids=[0])
    return r.results[0]["out_0_dram"]
```
